# Optimizing a Trainium2 kernel written in Bass

```python
import numpy as np
import jax
import jax.numpy as jnp

def _softmax(x, axis=-1):
    return jax.nn.softmax(x, axis=axis)

def _gelu(x):
    return jax.nn.gelu(x, approximate=True)

def _silu(x):
    return jax.nn.silu(x)

def _sigmoid(x):
    return jax.nn.sigmoid(x)

def _layernorm(x, axis=-1, eps=1e-05):
    m = jnp.mean(x, axis=axis, keepdims=True)
    v = jnp.var(x, axis=axis, keepdims=True)
    return (x - m) / jnp.sqrt(v + eps)

def _scatter_add(tgt, idx, src, axis=0):
    return tgt.at[idx].add(src)

def _segment_sum(src, seg, n):
    return jax.ops.segment_sum(src, seg, n)
kernel_name = 'mk_decoder_preln_d1_seqx_r2_2f8133'

def setup_inputs(seed: int=0):
    np.random.seed(seed)
    _w = jnp.asarray

    def _rec_inputs():
        import jax
        import jax.numpy as jnp
        _rk = jax.random.key(seed)
        x = 7.22e-05 + 1 * jax.random.normal(jax.random.fold_in(_rk, 1), (32, 256, 512), jnp.float32)
        _lenS = 256 - jax.random.randint(jax.random.fold_in(_rk, 7), (32,), 0, max(1, 256 // 4) + 1, jnp.int32)
        _lenS2 = 256 - jax.random.randint(jax.random.fold_in(_rk, 8), (32,), 0, max(1, 256 // 4) + 1, jnp.int32)
        _ctx_1024P = jax.random.normal(jax.random.fold_in(_rk, 11), (32, 16, 512), jnp.float32)
        _ctx_1024c = jax.random.dirichlet(jax.random.fold_in(_rk, 511), 0.3 * jnp.ones((16,), jnp.float32), (32, 256))
        _ctx_1024t = jnp.einsum('bsk,bkd->bsd', _ctx_1024c, _ctx_1024P)
        _ctx_1024t = _ctx_1024t * jax.lax.rsqrt(jnp.mean(jnp.square(_ctx_1024t)) + 1e-12) * 0.953939
        ctx_1024 = -0.000514642 + 1.00011 * (_ctx_1024t + 0.3 * jax.random.normal(jax.random.fold_in(_rk, 611), (32, 256, 512), jnp.float32))
        return (x, ctx_1024)
    x, ctx_1024 = _rec_inputs()

    def _L0_attn_setup():
        import jax, jax.numpy as jnp
        import numpy as np
        D_MODEL = 512
        N_HEAD = 16
        SEQ = 1024
        BATCH = 2
        key = jax.random.key(seed)
        x = jax.random.normal(key, (BATCH, SEQ, D_MODEL), dtype=jnp.float32)
        return {'x': x}
    _L0_attn_all = _L0_attn_setup()
    _L0_attn_in = {k: v for k, v in _L0_attn_all.items() if k in ()}
    del _L0_attn_all

    def _L0_xattn_setup():
        import jax, jax.numpy as jnp
        import numpy as np
        B, L_ENC, L_DEC, D = (16, 256, 128, 512)
        key = jax.random.key(seed)
        k1, k2, k3, k4, k5, k6 = jax.random.split(key, 6)
        encoder_hc = jax.random.normal(k1, (B, L_ENC, D), dtype=jnp.float32)
        decoder_hq = jax.random.normal(k2, (B, L_DEC, D), dtype=jnp.float32)
        w_sim = jax.random.normal(k3, (3 * D,), dtype=jnp.float32) * 0.02
        b_sim = jax.random.normal(k4, (1,), dtype=jnp.float32) * 0.02
        W_qv = jax.random.normal(k5, (4 * D, D), dtype=jnp.float32) * 0.02
        b_qv = jax.random.normal(k6, (D,), dtype=jnp.float32) * 0.02
        return {'encoder_hc': encoder_hc, 'decoder_hq': decoder_hq, 'w_sim': w_sim, 'b_sim': b_sim, 'W_qv': W_qv, 'b_qv': b_qv}
    _L0_xattn_all = _L0_xattn_setup()
    _L0_xattn_in = {k: v for k, v in _L0_xattn_all.items() if k in ('w_sim', 'b_sim', 'W_qv', 'b_qv')}
    del _L0_xattn_all

    def _L0_ffn_setup():
        import jax, jax.numpy as jnp
        import numpy as np
        DIM = 512

        def _reference_tuple_inner(x, W_r, W_k, W_v, mu_r, mu_k):
            B, T, C = x.shape
            x_prev = jnp.concatenate([jnp.zeros((B, 1, C), x.dtype), x[:, :-1, :]], axis=1)
            xr = mu_r * x + (1.0 - mu_r) * x_prev
            xk = mu_k * x + (1.0 - mu_k) * x_prev
            r = jax.nn.sigmoid(jnp.einsum('btc,dc->btd', xr, W_r))
            k = jnp.einsum('btc,dc->btd', xk, W_k)
            k_act = jnp.square(jax.nn.relu(k))
            out = r * jnp.einsum('btc,dc->btd', k_act, W_v)
            new_state = x[:, -1, :]
            return (out, new_state)
        key = jax.random.key(seed)
        ks = jax.random.split(key, 6)
        B, T, C = (8, 1024, DIM)
        x = jax.random.normal(ks[0], (B, T, C), dtype=jnp.float32)
        s = 1.0 / np.sqrt(C)
        W_r = jax.random.uniform(ks[1], (C, C), jnp.float32, -s, s)
        W_k = jax.random.uniform(ks[2], (C, C), jnp.float32, -s, s)
        W_v = jax.random.uniform(ks[3], (C, C), jnp.float32, -s, s)
        mu_r = jax.random.uniform(ks[4], (C,), jnp.float32)
        mu_k = jax.random.uniform(ks[5], (C,), jnp.float32)
        return {'x': x, 'W_r': W_r, 'W_k': W_k, 'W_v': W_v, 'mu_r': mu_r, 'mu_k': mu_k}
    _L0_ffn_all = _L0_ffn_setup()
    _L0_ffn_in = {k: v for k, v in _L0_ffn_all.items() if k in ('W_r', 'W_k', 'W_v', 'mu_r', 'mu_k')}
    del _L0_ffn_all
    return {'x': x, 'ctx_1024': ctx_1024, 'L0_xattn_w_sim': _L0_xattn_in['w_sim'], 'L0_xattn_b_sim': _L0_xattn_in['b_sim'], 'L0_xattn_W_qv': _L0_xattn_in['W_qv'], 'L0_xattn_b_qv': _L0_xattn_in['b_qv'], 'L0_ffn_W_r': _L0_ffn_in['W_r'], 'L0_ffn_W_k': _L0_ffn_in['W_k'], 'L0_ffn_W_v': _L0_ffn_in['W_v'], 'L0_ffn_mu_r': _L0_ffn_in['mu_r'], 'L0_ffn_mu_k': _L0_ffn_in['mu_k']}

def reference(x, ctx_1024, L0_xattn_w_sim, L0_xattn_b_sim, L0_xattn_W_qv, L0_xattn_b_qv, L0_ffn_W_r, L0_ffn_W_k, L0_ffn_W_v, L0_ffn_mu_r, L0_ffn_mu_k):
    import jax
    import jax.numpy as jnp

    def _L0_attn_ref(x):
        import jax, jax.numpy as jnp
        import numpy as np
        D_MODEL = 512
        N_HEAD = 16
        SEQ = 1024
        BATCH = 2
        B, S, D = x.shape
        H = N_HEAD
        hd = D // H
        qkv = x.reshape(B, S, H, hd).transpose(0, 2, 1, 3)
        q = k = v = qkv
        w = jnp.einsum('bhqd,bhkd->bhqk', q, k) / jnp.sqrt(jnp.asarray(hd, x.dtype))
        causal = jnp.tril(jnp.ones((S, S), dtype=bool))
        mask_value = jnp.finfo(w.dtype).min
        w = jnp.where(causal[None, None, :, :], w, mask_value)
        w = jax.nn.softmax(w, axis=-1)
        out = jnp.einsum('bhqk,bhkd->bhqd', w, v)
        return out.transpose(0, 2, 1, 3).reshape(B, S, D)

    def _L0_xattn_ref(encoder_hc, decoder_hq, w_sim, b_sim, W_qv, b_qv):
        import jax, jax.numpy as jnp
        import numpy as np
        B, L_ENC, L_DEC, D = (16, 256, 128, 512)
        d = encoder_hc.shape[-1]
        w1, w2, w3 = (w_sim[:d], w_sim[d:2 * d], w_sim[2 * d:])
        Sim = (encoder_hc @ w1)[:, :, None] + (decoder_hq @ w2)[:, None, :] + jnp.einsum('bid,bjd->bij', encoder_hc * w3, decoder_hq) + b_sim[0]
        A = jax.nn.softmax(Sim, axis=2)
        hq_hat = jnp.einsum('bij,bjd->bid', A, decoder_hq)
        Batt = jax.nn.softmax(jnp.max(Sim, axis=2), axis=1)
        hc_bar = jnp.einsum('bi,bid->bd', Batt, encoder_hc)[:, None, :]
        hc_hat = jnp.broadcast_to(hc_bar, encoder_hc.shape)
        feats = jnp.concatenate([encoder_hc, hq_hat, encoder_hc * hq_hat, encoder_hc * hc_hat], axis=-1)
        hcq = feats @ W_qv + b_qv
        return hcq

    def _L0_ffn_ref(x, W_r, W_k, W_v, mu_r, mu_k):
        import jax, jax.numpy as jnp
        import numpy as np
        DIM = 512

        def _reference_tuple_inner(x, W_r, W_k, W_v, mu_r, mu_k):
            B, T, C = x.shape
            x_prev = jnp.concatenate([jnp.zeros((B, 1, C), x.dtype), x[:, :-1, :]], axis=1)
            xr = mu_r * x + (1.0 - mu_r) * x_prev
            xk = mu_k * x + (1.0 - mu_k) * x_prev
            r = jax.nn.sigmoid(jnp.einsum('btc,dc->btd', xr, W_r))
            k = jnp.einsum('btc,dc->btd', xk, W_k)
            k_act = jnp.square(jax.nn.relu(k))
            out = r * jnp.einsum('btc,dc->btd', k_act, W_v)
            new_state = x[:, -1, :]
            return (out, new_state)
        return _reference_tuple_inner(x, W_r, W_k, W_v, mu_r, mu_k)[0]
    x = x + _L0_attn_ref(_layernorm(x, axis=-1))
    x = x + _L0_xattn_ref(_layernorm(x, axis=-1), ctx_1024, L0_xattn_w_sim, L0_xattn_b_sim, L0_xattn_W_qv, L0_xattn_b_qv)
    x = x + _L0_ffn_ref(_layernorm(x, axis=-1), L0_ffn_W_r, L0_ffn_W_k, L0_ffn_W_v, L0_ffn_mu_r, L0_ffn_mu_k)
    return x

_drawn_inputs = setup_inputs


def setup_inputs(seed=0):
    import zlib

    import numpy as np

    out = dict(_drawn_inputs(seed))
    spreads = {}
    factors = {'L0_xattn_b_qv': 4.996, 'L0_ffn_W_r': 5.62, 'L0_ffn_mu_r': 8.0}
    for name, (base, spread) in spreads.items():
        noise = np.random.default_rng([zlib.crc32(name.encode()), seed]).standard_normal(out[name].shape)
        drawn = base * np.exp(spread * noise) if base else spread * noise
        out[name] = jnp.asarray(drawn.astype(out[name].dtype))
    for name, factor in factors.items():
        out[name] = (out[name] * factor).astype(out[name].dtype)
    return out
```

```python
from contextlib import ExitStack

import concourse.bass as bass
from concourse import mybir

ACT = mybir.ActivationFunctionType
ALU = mybir.AluOpType
AX = mybir.AxisListType
F32 = mybir.dt.float32
F32R = mybir.dt.float32r

P = 128
B, S, D = 32, 256, 512
H = 16
HD = D // H
TT = S // P
C = D // P
G = C
R = H // G
EPS = 1e-5
SCALE = HD ** -0.5
SHIFT = D * SCALE / 2

MERGE_ORDER = [2, 3, 0, 1]

LATE = {"pre": -1, "att": 0, "xa": 1, "ffn": 2}
FILLS = {
    "T0": [("eT0", "xa"), ("cT0", "xa"), ("yT0", "ffn"), ("sim", "xa"), ("aT", "xa"), ("ub", "xa"),
           ("xT0", "pre")],
    "T1": [("eT1", "xa"), ("cT1", "xa"), ("yT1", "ffn"), ("pv0", "att"), ("pv1", "att"),
           ("pv2", "att"), ("pv3", "att"), ("xT1", "pre")],
    "D0": [("k0", "ffn"), ("r0", "ffn"), ("r1", "ffn"), ("hq0", "xa"), ("h0", "xa")],
    "D1": [("k1", "ffn"), ("v0", "ffn"), ("v1", "ffn"), ("hq1", "xa"), ("h1", "xa")],
}
BANK = {name: bank for bank, fills in FILLS.items() for name, _ in fills}
BANKS = list(FILLS)
TMP_USES = [("ew", "xa", "ew", 2, 2), ("xr", "ffn", "xr", 2, 2), ("ka", "ffn", "ka", 2, 2), ("hc", "xa", "hc", C, C),
            ("weff", "xa", "weff", C // 2, C), ("eh", "xa", "eh", 2, 2), ("weff_rest", "xa", "weff", C, C),
            ("e_w1", "att", "e_w1", TT, TT)]
SETUP_FILLS = 3


def fill_number(name, i):
    fills = FILLS[BANK[name]]
    at = [f for f, _ in fills].index(name)
    through = [LATE[stage] - (n <= at) for n, (_, stage) in enumerate(fills)]
    if isinstance(i, int):
        return SETUP_FILLS + sum(min(max(i - late, 0), B) for late in through)
    return i * len(fills) + (SETUP_FILLS - sum(through))


def build(nc, x, ctx_in, w_sim, b_sim, w_qv, b_qv, w_r, w_k, w_v, mu_r, mu_k, out):
    with ExitStack() as stack:
        def sb(name, shape, dt=F32):
            return stack.enter_context(nc.sbuf_tensor(name, shape, dt))

        def sem(name):
            return stack.enter_context(nc.semaphore(name))

        ident = sb("ident", [P, P])
        neg_half = sb("neg_half", [P, TT])
        neg_shift = sb("neg_shift", [P, 1])
        w1_row = sb("w1_row", [P, D])
        b_sim_col = sb("b_sim_col", [P, 1])
        b_row = sb("b_row", [P, D])
        w2_col = sb("w2_col", [P, C])
        w3_col = sb("w3_col", [P, C])
        mu = {"xk": sb("mu_k_col", [P, C]), "xr": sb("mu_r_col", [P, C])}
        one_less_mu = {"xk": sb("one_less_mu_k", [P, C]), "xr": sb("one_less_mu_r", [P, C])}
        wqv1 = sb("wqv1", [P, C, D])
        wqv4 = sb("wqv4", [P, C, D])
        wqv2 = [sb(f"wqv2_{h}", [P, C, D], F32R) for h in ("hi", "lo")]
        wqv3 = [sb(f"wqv3_{h}", [P, C, D], F32R) for h in ("hi", "lo")]
        wT = {n: [sb(f"{n}_{h}", [P, C, D], F32R) for h in ("hi", "lo")] for n in ("wrT", "wkT", "wvT")}

        ctx_sb = sb("ctx_sb", [P, TT, D])
        xn = sb("xn", [P, TT, D + HD])
        x1 = sb("x1", [P, TT, D])
        x1b = sb("x1b", [P, TT, D])
        e = sb("e", [P, TT, D])
        x2 = sb("x2", [P, TT, D])
        y = sb("y", [P, TT, D])
        x_in = e
        a = sb("a", [P, TT, S])
        probs = sb("probs", [P, R, 3 * P])
        pv_scaled = sb("pv_scaled", [P, TT, R, HD])
        tmp = [sb(f"tmp{n}", [P, D]) for n in range(2)]
        eTf = sb("eTf", [P, C, S])
        eT = [sb(f"eT_{h}", [P, C, S], F32R) for h in ("hi", "lo")]
        xT = [sb(f"xT_{h}", [P, C, S], F32R) for h in ("hi", "lo")]
        yT = sb("yT", [P, C, S + 1])
        area_c = sb("area_c", [P, 2 * C * S], F32R)
        area_k = sb("area_k", [P, 2 * C * S], F32R)
        area_e = sb("area_e", [P, 2 * C * S], F32R)
        area_x = sb("area_x", [P, 2 * C * S], F32R)
        area_m = sb("area_m", [P, 2 * C * S], F32R)

        def pair(area, n, width, base=0, step=C * S):
            return [area[:, base + h * step:base + h * step + n * width].rearrange("p (c s) -> p c s", c=n)
                    for h in range(2)]

        cT, kaT, ewT, ehT = (pair(t, C, S) for t in (area_c, area_k, area_e, area_e))
        xrT, hqT, xkT = (pair(t, C, S) for t in (area_x, area_x, area_m))
        c_rows = pair(area_m, TT, D)
        aT = pair(area_c, TT, S, step=TT * S)
        weff = [pair((area_c, area_k)[c // 2], 1, D, base=(c % 2) * D) for c in range(C)]

        stats = {n: sb(f"stats_{n}", [P, TT, 6]) for n in "xey"}
        moments = {n: sb(f"moments_{n}", [P, TT, 2]) for n in "xey"}
        var = {n: sb(f"var_{n}", [P, TT]) for n in "xey"}
        rstd = {n: sb(f"rstd_{n}", [P, TT]) for n in "xey"}
        r_den = sb("r_den", [P, G, TT, R])
        e_w1 = sb("e_w1", [P, TT])
        neg_max = sb("neg_max", [P, TT])
        a_sum = sb("a_sum", [P, TT])
        a_rsum = sb("a_rsum", [P, TT])
        u = sb("u", [P, TT])
        ub_neg_max = sb("ub_neg_max", [P, 1])
        ub_sum = sb("ub_sum", [P, 1])
        ub_rsum = sb("ub_rsum", [P, 1])
        batt = a[:, 0, :]
        hc = sb("hc", [P, C])

        ps = {n: stack.enter_context(nc.psum_tensor(n, [P, D], F32)) for n in BANKS}
        ps_scores = stack.enter_context(nc.psum_tensor("ps_scores", [P, R, D], F32))

        filled = {n: sem(f"filled_{n}") for n in BANKS}
        drained = {n: sem(f"drained_{n}") for n in BANKS}

        x_loaded, ctx_loaded, x1_loaded, out_stored = map(sem, ("x_loaded", "ctx_loaded", "x1_loaded", "out_stored"))
        small_loaded, w_turned, w_split, wqv_loaded = map(sem, ("small_loaded", "w_turned", "w_split", "wqv_loaded"))
        stage_loaded = [sem(f"stage_loaded_{n}") for n in range(4)]
        w_hi, consts_ready, ident_zero, mu_less, yT_zero = map(
            sem, ("w_hi", "consts_ready", "ident_zero", "mu_less", "yT_zero"))
        stats_done = {n: sem(f"stats_done_{n}") for n in "xey"}
        moments_done = {n: sem(f"moments_done_{n}") for n in "xey"}
        var_done = {n: sem(f"var_done_{n}") for n in "xey"}
        rstd_done = {n: sem(f"rstd_done_{n}") for n in "xey"}
        normed = {n: sem(f"normed_{n}") for n in "xey"}
        scores_ready, probs_ready, probs_masked = map(sem, ("scores_ready", "probs_ready", "probs_masked"))
        den_ready, pv_scaled_ready, x1_ready, x1b_ready = map(
            sem, ("den_ready", "pv_scaled_ready", "x1_ready", "x1b_ready"))
        eT_hi, eT_split, cT_hi, xT_hi, aT_hi, hqT_hi = map(
            sem, ("eT_hi", "eT_split", "cT_hi", "xT_hi", "aT_hi", "hqT_hi"))
        KINDS = ("ew", "xk", "xr", "ka", "eh", "weff")
        f_ready = {n: sem(f"{n}_f") for n in KINDS}
        hi_ready = {n: sem(f"{n}_hi") for n in KINDS}
        split = {n: sem(f"{n}_split") for n in KINDS}
        prev_scaled = {n: sem(f"{n}_prev_scaled") for n in ("xk", "xr")}
        ctx_hi, ctx_split = sem("ctx_hi"), sem("ctx_split")
        pool_passed, dve_passed, sp_passed = map(sem, ("pool_passed", "dve_passed", "sp_passed"))
        out_ready = sem("out_ready")
        neg_max_ready, a_exp, a_rsum_ready, a_normed, e_w1_ready, u_ready = map(
            sem, ("neg_max_ready", "a_exp", "a_rsum_ready", "a_normed", "e_w1_ready", "u_ready"))
        ub_max_ready, batt_ready, ub_rsum_ready, hc_ready = map(
            sem, ("ub_max_ready", "batt_ready", "ub_rsum_ready", "hc_ready"))

        def wait(eng, semaphore, value):
            if not isinstance(value, int) or value > 0:
                eng.wait_ge(semaphore, value)

        def wait_filled(eng, name, i):
            eng.wait_ge(filled[BANK[name]], fill_number(name, i))

        def wait_drained(eng, name, i):
            eng.wait_ge(drained[BANK[name]], fill_number(name, i))

        def stages(i):
            return {n for n, late in LATE.items() if 0 <= i - late < B}

        def wait_tmp(eng, kind, i):
            tmp_used = {**split, "hc": hc_ready, "e_w1": e_w1_ready}
            at = [use[0] for use in TMP_USES].index(kind)
            for n in range(at - 1, at - 1 - len(TMP_USES), -1):
                _, stage_name, count, upto, per = TMP_USES[n]
                j = i - (n < 0)
                if not isinstance(i, int) or stage_name in stages(j):
                    eng.wait_ge(tmp_used[count], per * (j - LATE[stage_name]) + upto)
                    return

        value_of = {n: [t[:] for t in tmp] for n in ("ew", "xr", "ka", "eh")}
        value_of["xk"] = [y[:, h, :] for h in range(2)]

        def half(bank_ap):
            return bank_ap.rearrange("p (c s) -> p c s", c=2)

        def steps(eng, step):
            first = max(LATE.values())
            last = B - 1 + min(LATE.values())
            for i in range(min(LATE.values()), first):
                step(i, stages(i))
            with eng.Fori(first, last + 1) as i:
                step(i, set(LATE))
            for i in range(last + 1, B + max(LATE.values())):
                step(i, stages(i))

        stage = [x1, x1b, e, x2]
        staged = [(n, h) for n in ("wkT", "wrT", "wvT", "wqv2", "wqv3") for h in range(2)]

        def wait_staged(eng, n):
            eng.wait_ge(stage_loaded[n % len(stage)], 16 * (n // len(stage) + 1))

        def wait_stage_free(eng):
            eng.wait_ge(w_turned, 3)
            eng.wait_ge(w_split, len(staged) - 6)

        block = stack.enter_context(nc.Block())

        @block.sync
        def _(sp):
            xv = x.rearrange("b (t p) d -> b p t d", p=P)
            cv = ctx_in.rearrange("b (t p) d -> b p t d", p=P)
            ov = out.rearrange("b (t p) d -> b p t d", p=P)
            wqv = w_qv.rearrange("(q h c p) d -> q h p c d", q=4, h=2, p=P)
            dram = {"wkT": w_k, "wrT": w_r, "wvT": w_v}
            for n, (name, h) in enumerate(staged):
                if n >= len(stage):
                    sp.wait_ge(w_turned, (n - len(stage)) // 2 + 1)
                src = wqv[int(name[-1]) - 1, h] if name in ("wqv2", "wqv3") else \
                    dram[name].rearrange("(h c p) d -> h p c d", h=2, p=P)[h]
                sp.dma_start(stage[n % len(stage)][:], src).then_inc(stage_loaded[n % len(stage)], 16)
                if n == 3:
                    sp.dma_start(ctx_sb[:], cv[0]).then_inc(ctx_loaded, 16)
            for h in range(2):
                sp.dma_start(wqv1[:, 2 * h:2 * h + 2, :], wqv[0, h]).then_inc(wqv_loaded, 16)
                sp.dma_start(wqv4[:, 2 * h:2 * h + 2, :], wqv[3, h]).then_inc(wqv_loaded, 16)

            def step(i, on):
                p, n, m, l = i + 1, i, i - 1, i - 2
                if "pre" in on:
                    if "xa" in on:
                        wait_filled(sp, "eT1", i)
                        sp.sem_inc(sp_passed, 1)
                        sp.wait_ge(e_w1_ready, TT * (m + 1))
                    elif p:
                        sp.wait_ge(normed["x"], TT * p)
                    else:
                        wait_stage_free(sp)
                    sp.dma_start(x_in[:], xv[p]).then_inc(x_loaded, 16)
                if "att" in on:
                    if isinstance(n, int) and n == 0:
                        wait_stage_free(sp)
                    wait(sp, normed["e"], TT * n)
                    wait(sp, x1b_ready, n)
                    sp.dma_start(x1[:], xv[n]).then_inc(x1_loaded, 16)
                if "xa" in on and not (isinstance(m, int) and m == B - 1):
                    sp.wait_ge(ctx_split, m + 1)
                    sp.dma_start(ctx_sb[:], cv[m + 1]).then_inc(ctx_loaded, 16)
                if "ffn" in on:
                    for t in range(TT):
                        sp.wait_ge(out_ready, TT * l + t + 1)
                        sp.dma_start(ov[l][:, t], x2[:, t, :]).then_inc(out_stored, 16)

            steps(sp, step)
            sp.wait_ge(out_stored, 16 * TT * B)

        @block.gpsimd
        def _(pool):
            pool.memset(ident[:], 0.0).then_inc(ident_zero, 1)
            pool.memset(neg_half[:], -0.5).then_inc(consts_ready, 1)
            pool.memset(neg_shift[:], -SHIFT).then_inc(consts_ready, 1)
            pool.memset(xn[:, :, D:], 1.0).then_inc(consts_ready, 1)
            pool.memset(yT[:, :, 0:1], 0.0).then_inc(consts_ready, 1)
            pool.wait_ge(ident_zero, 1)
            pool.affine_select(out=ident[:], in_=ident[:], compare_op=ALU.not_equal, fill=1.0, base=0,
                               pattern=[[-1, P]], channel_multiplier=1).then_inc(consts_ready, 1)
            pool.dma_start(w2_col[:], w_sim[D:2 * D].rearrange("(c p) -> p c", p=P),
                           allow_slow_non_contiguous=True).then_inc(small_loaded, 16)
            pool.dma_start(w3_col[:], w_sim[2 * D:3 * D].rearrange("(c p) -> p c", p=P),
                           allow_slow_non_contiguous=True).then_inc(small_loaded, 16)
            pool.dma_start(mu["xr"][:], mu_r.rearrange("(c p) -> p c", p=P),
                           allow_slow_non_contiguous=True).then_inc(small_loaded, 16)
            pool.dma_start(mu["xk"][:], mu_k.rearrange("(c p) -> p c", p=P),
                           allow_slow_non_contiguous=True).then_inc(small_loaded, 16)
            pool.dma_start(w1_row[:], w_sim[0:D].partition_broadcast(P)).then_inc(small_loaded, 16)
            pool.dma_start(b_row[:], b_qv.partition_broadcast(P)).then_inc(small_loaded, 16)
            pool.dma_start(b_sim_col[:], b_sim.partition_broadcast(P)).then_inc(small_loaded, 16)
            pool.wait_ge(small_loaded, 7 * 16)
            pool.wait_ge(consts_ready, 5)

            def root(n, b):
                pool.wait_ge(var_done[n], b + 1)
                pool.tensor_tensor(rstd[n][:], var[n][:], neg_half[:], ALU.pow).then_inc(rstd_done[n], 1)

            def mask(n, g):
                pool.wait_ge(probs_ready, G * n + g + 1)
                pool.sem_inc(pool_passed, 1)
                for k in range(TT):
                    diag = probs[:, :, 2 * k * P:(2 * k + 1) * P]
                    last = pool.affine_select(out=diag, in_=diag, compare_op=ALU.is_ge, fill=0.0, base=0,
                                              pattern=[[0, R], [1, P]], channel_multiplier=-1)
                last.then_inc(probs_masked, 1)

            def add_out(i, l, t):
                wait_drained(pool, f"v{t}", i)
                pool.tensor_tensor(x2[:, t, :], x2[:, t, :], y[:, t, :], ALU.add).then_inc(out_ready, 1)

            def step(i, on):
                p, n, m, l = i + 1, i, i - 1, i - 2
                if "att" in on:
                    mask(n, 0)
                if "xa" in on:
                    pool.wait_ge(x1_ready, G * (m + 1))
                    if isinstance(m, int) and m == 0:
                        wait_stage_free(pool)
                    else:
                        wait_drained(pool, "h0", i - 1)
                        wait_drained(pool, "h1", i - 1)
                    for t in range(TT):
                        last = pool.tensor_tensor(x1b[:, t, :], x1[:, t, :], b_row[:], ALU.add)
                    last.then_inc(x1b_ready, 1)
                if "att" in on:
                    mask(n, 1)
                if "xa" in on:
                    for h in range(2):
                        pool.wait_ge(eT_hi, 2 * m + h + 1)
                        pool.tensor_tensor(eT[1][:, 2 * h:2 * h + 2, :], eTf[:, 2 * h:2 * h + 2, :],
                                           eT[0][:, 2 * h:2 * h + 2, :].bitcast(F32), ALU.subtract)\
                            .then_inc(eT_split, 1)
                    pool.wait_ge(ctx_loaded, 16 * (m + 1))
                    wait_filled(pool, "cT1", i)
                    if "ffn" in on:
                        wait_filled(pool, "k1", i)
                    pool.sem_inc(pool_passed, 1)
                    for t in range(TT):
                        last = pool.tensor_scalar(c_rows[0][:, t, :], ctx_sb[:, t, :], 1.0, 0.0, ALU.mult, ALU.add)
                    last.then_inc(ctx_hi, 1)
                    pool.wait_ge(ctx_hi, m + 1)
                    for t in range(TT):
                        last = pool.tensor_tensor(c_rows[1][:, t, :], ctx_sb[:, t, :],
                                                  c_rows[0][:, t, :].bitcast(F32), ALU.subtract)
                    last.then_inc(ctx_split, 1)
                if "att" in on:
                    mask(n, 2)
                if "pre" in on:
                    root("x", p)
                if "ffn" in on:
                    add_out(i, l, 0)
                if "att" in on:
                    mask(n, 3)
                if "ffn" in on:
                    add_out(i, l, 1)
                if "att" in on:
                    root("e", n)
                if "xa" in on:
                    root("y", m)

            steps(pool, step)

        @block.scalar
        def _(act):
            def copy(dst, src):
                return act.activation(dst, src, ACT.Copy)

            done = 0
            for n, name in enumerate(("wkT", "wrT", "wvT")):
                for kc in range(C):
                    bank = BANKS[kc]
                    act.wait_ge(filled[bank], n + 1)
                    act.activation(wT[name][0][:, kc, :], ps[bank][:], ACT.Copy,
                                   scale=0.5 if name == "wvT" else 1.0).then_inc(w_hi, 1)
            for n in range(6, len(staged)):
                name, h = staged[n]
                dst = (wqv2 if name == "wqv2" else wqv3)[0]
                wait_staged(act, n)
                copy(dst[:, 2 * h:2 * h + 2, :], stage[n % len(stage)][:]).then_inc(w_hi, 1)
            act.wait_ge(consts_ready, 5)
            act.wait_ge(mu_less, 2)

            def exp_scores(n, g):
                act.wait_ge(scores_ready, G * n + g + 1)
                if g:
                    wait_filled(act, f"pv{g - 1}", n)
                elif not isinstance(n, int) or n > 0:
                    wait_filled(act, f"pv{G - 1}", n - 1)
                act.activation(probs[:], ps_scores[:, :, 0:3 * P], ACT.Exp, bias=neg_shift[:], scale=SCALE)\
                    .then_inc(probs_ready, 1)

            def split_hi(kind, dst, b):
                for h in range(2):
                    act.wait_ge(f_ready[kind], 2 * b + h + 1)
                    copy(dst[0][:, 2 * h:2 * h + 2, :], half(value_of[kind][h])).then_inc(hi_ready[kind], 1)

            def scale_prev(kind):
                for h in range(2):
                    for c in range(2 * h, 2 * h + 2):
                        last = act.activation(half(value_of[kind][h])[:, c % 2, :], yT[:, c, 0:S], ACT.Copy,
                                              scale=one_less_mu[kind][:, c:c + 1])
                    last.then_inc(prev_scaled[kind], 1)

            def psum_hi(name, dst, done, i):
                for h in range(2):
                    wait_filled(act, f"{name}{h}", i)
                    copy(dst[0][:, 2 * h:2 * h + 2, :], half(ps[BANK[f"{name}{h}"]][:])).then_inc(done, 1)

            def step(i, on):
                p, n, m, l = i + 1, i, i - 1, i - 2
                def merged_hi(at):
                    act.wait_ge(f_ready["weff"], C * m + at + 1)
                    copy(weff[MERGE_ORDER[at]][0][:, 0, :], tmp[at % 2][:]).then_inc(hi_ready["weff"], 1)

                def tanh(t):
                    wait_filled(act, f"r{t}", i)
                    act.activation(y[:, t, :], ps[BANK[f"r{t}"]][:], ACT.Tanh, scale=0.5)\
                        .then_inc(drained[BANK[f"r{t}"]], 1)

                if "xa" in on:
                    for h in range(2):
                        wait_filled(act, f"eT{h}", i)
                        copy(eTf[:, 2 * h:2 * h + 2, :], half(ps[BANK[f"eT{h}"]][:]))\
                            .then_inc(drained[BANK[f"eT{h}"]], 1)
                if "att" in on:
                    exp_scores(n, 0)
                if "xa" in on:
                    psum_hi("cT", cT, cT_hi, i)
                    split_hi("ew", ewT, m)
                if "ffn" in on:
                    for h in range(2):
                        wait_filled(act, f"yT{h}", i)
                        copy(yT[:, 2 * h:2 * h + 2, 1:], half(ps[BANK[f"yT{h}"]][:]))\
                            .then_inc(drained[BANK[f"yT{h}"]], 1)
                    wait_drained(act, "yT1", i)
                    scale_prev("xk")
                    split_hi("xk", xkT, l)
                if "att" in on:
                    exp_scores(n, 1)
                if "ffn" in on:
                    wait_tmp(act, "xr", i)
                    scale_prev("xr")
                if "xa" in on:
                    wait_filled(act, "sim", i)
                    act.wait_ge(neg_max_ready, m + 1)
                    for t in range(TT):
                        last = act.activation(a[:, t, :], ps["T0"][:, t * S:(t + 1) * S], ACT.Exp,
                                              bias=neg_max[:, t:t + 1], accum_out=a_sum[:, t:t + 1])
                        last.then_inc(a_exp if t == 0 else drained[BANK["sim"]], 1)
                    wait_drained(act, "eT1", i)
                    for h in range(2):
                        copy(eT[0][:, 2 * h:2 * h + 2, :], eTf[:, 2 * h:2 * h + 2, :]).then_inc(eT_hi, 1)
                if "ffn" in on:
                    split_hi("xr", xrT, l)
                    for h in range(2):
                        wait_filled(act, f"k{h}", i)
                        act.activation(y[:, h, :], ps[BANK[f"k{h}"]][:], ACT.Relu).then_inc(drained[BANK[f"k{h}"]], 1)
                    split_hi("ka", kaT, l)
                if "att" in on:
                    exp_scores(n, 2)
                if "ffn" in on:
                    tanh(0)
                if "xa" in on:
                    wait_filled(act, "aT", i)
                    copy(aT[0], half(ps[BANK["aT"]][:])).then_inc(aT_hi, 1)
                if "ffn" in on:
                    tanh(1)
                if "att" in on:
                    exp_scores(n, 3)
                if "xa" in on:
                    act.wait_ge(ub_max_ready, m + 1)
                    act.activation(batt, ps[BANK["ub"]][:, 0:S], ACT.Exp, bias=ub_neg_max[:],
                                   accum_out=ub_sum[:]).then_inc(drained[BANK["ub"]], 1)
                    merged_hi(0)
                    merged_hi(1)
                    psum_hi("hq", hqT, hqT_hi, i)
                    for h in range(2):
                        wait_drained(act, f"hq{h}", i)
                        copy(ehT[0][:, 2 * h:2 * h + 2, :], half(tmp[h][:])).then_inc(hi_ready["eh"], 1)
                    merged_hi(2)
                    merged_hi(3)
                if "pre" in on:
                    psum_hi("xT", xT, xT_hi, i)

            steps(act, step)

        @block.vector
        def _(dve):
            n_hi = 0
            for n, name in enumerate(("wkT", "wrT", "wvT")):
                for kc in range(C):
                    bank = BANKS[kc]
                    n_hi += 1
                    dve.wait_ge(w_hi, n_hi)
                    dve.scalar_tensor_tensor(wT[name][1][:, kc, :], ps[bank][:], 0.5 if name == "wvT" else 1.0,
                                             wT[name][0][:, kc, :].bitcast(F32), ALU.mult, ALU.subtract)\
                        .then_inc(drained[bank], 1)
            for n in range(6, len(staged)):
                name, h = staged[n]
                dst = wqv2 if name == "wqv2" else wqv3
                n_hi += 1
                dve.wait_ge(w_hi, n_hi)
                dve.tensor_tensor(dst[1][:, 2 * h:2 * h + 2, :], stage[n % len(stage)][:],
                                  dst[0][:, 2 * h:2 * h + 2, :].bitcast(F32), ALU.subtract).then_inc(w_split, 1)
            dve.wait_ge(small_loaded, 7 * 16)
            dve.wait_ge(wqv_loaded, 4 * 16)
            wait_stage_free(dve)
            for n in ("xk", "xr"):
                dve.tensor_scalar(one_less_mu[n][:], mu[n][:], -1.0, 1.0, ALU.mult, ALU.add).then_inc(mu_less, 1)
            dve.wait_ge(mu_less, 2)

            def psum_lo(name, dst, done, per, b, i):
                for h in range(2):
                    bank = BANK[f"{name}{h}"]
                    dve.wait_ge(done, per * b + h + 1)
                    dve.tensor_tensor(dst[1][:, 2 * h:2 * h + 2, :], half(ps[bank][:]),
                                      dst[0][:, 2 * h:2 * h + 2, :].bitcast(F32), ALU.subtract)\
                        .then_inc(drained[bank], 1)

            def split_lo(kind, dst, b):
                for h in range(2):
                    dve.wait_ge(hi_ready[kind], 2 * b + h + 1)
                    dve.tensor_tensor(dst[1][:, 2 * h:2 * h + 2, :], half(value_of[kind][h]),
                                      dst[0][:, 2 * h:2 * h + 2, :].bitcast(F32), ALU.subtract)\
                        .then_inc(split[kind], 1)

            def layernorm_stats(n, src, b):
                for t in range(TT):
                    dve.bn_stats(stats[n][:, t, :], src[:, t, :]).then_inc(stats_done[n], 1)
                dve.wait_ge(stats_done[n], TT * (b + 1))
                dve.sem_inc(dve_passed, 1)
                for t in range(TT):
                    dve.bn_aggr(moments[n][:, t, :], stats[n][:, t, :]).then_inc(moments_done[n], 1)
                dve.wait_ge(moments_done[n], TT * (b + 1))
                dve.tensor_scalar(var[n][:], moments[n][:, :, 1], EPS, None, ALU.add).then_inc(var_done[n], 1)

            def normalise(n, dst, src, b):
                dve.wait_ge(rstd_done[n], b + 1)
                for t in range(TT):
                    dve.tensor_scalar(dst(t), src(t), moments[n][:, t, 0:1], rstd[n][:, t:t + 1],
                                      ALU.subtract, ALU.mult).then_inc(normed[n], 1)

            def mix(kind, b):
                for h in range(2):
                    dve.wait_ge(prev_scaled[kind], 2 * b + h + 1)
                    for c in range(2 * h, 2 * h + 2):
                        part = half(value_of[kind][h])[:, c % 2, :]
                        last = dve.scalar_tensor_tensor(part, yT[:, c, 1:], mu[kind][:, c:c + 1], part,
                                                        ALU.mult, ALU.add)
                    last.then_inc(f_ready[kind], 1)

            def scale_values(n, g):
                wait_filled(dve, f"pv{g}", n)
                o = ps["T1"][:].rearrange("p (t r d) -> p t r d", t=TT, r=R)
                dve.reciprocal(r_den[:, g, :, :], o[:, :, :, HD]).then_inc(den_ready, 1)
                wait(dve, x1_ready, G * n + g)
                dve.wait_ge(den_ready, G * n + g + 1)
                dve.tensor_tensor(pv_scaled[:], o[:, :, :, 0:HD],
                                  r_den[:, g, :, :].unsqueeze(3).to_broadcast([P, TT, R, HD]), ALU.mult)\
                    .then_inc(drained[BANK[f"pv{g}"]], 1)

            def add_values(n, g):
                wait_drained(dve, f"pv{g}", n)
                if g == 0:
                    dve.wait_ge(x1_loaded, 16 * (n + 1))
                part = x1[:, :, g * P:(g + 1) * P].rearrange("p t (r d) -> p t r d", r=R)
                dve.tensor_tensor(part, part, pv_scaled[:], ALU.add).then_inc(x1_ready, 1)

            def attend(n, g):
                scale_values(n, g)
                add_values(n, g)

            def step(i, on):
                p, n, m, l = i + 1, i, i - 1, i - 2

                def gate(t):
                    wait_filled(dve, f"v{t}", i)
                    wait_drained(dve, f"r{t}", i)
                    dve.scalar_tensor_tensor(y[:, t, :], y[:, t, :], 1.0, ps[BANK[f"v{t}"]][:], ALU.add, ALU.mult)\
                        .then_inc(drained[BANK[f"v{t}"]], 1)

                def merge(at):
                    c = MERGE_ORDER[at]
                    dve.scalar_tensor_tensor(tmp[at % 2][:], wqv4[:, c, :], hc[:, c:c + 1], wqv1[:, c, :],
                                             ALU.mult, ALU.add).then_inc(f_ready["weff"], 1)

                def merged_lo(at):
                    dst = weff[MERGE_ORDER[at]]
                    dve.wait_ge(hi_ready["weff"], C * m + at + 1)
                    dve.tensor_tensor(dst[1][:, 0, :], tmp[at % 2][:], dst[0][:, 0, :].bitcast(F32),
                                      ALU.subtract).then_inc(split["weff"], 1)

                if "xa" in on:
                    wait_tmp(dve, "ew", i)
                    for h in range(2):
                        wait_drained(dve, f"eT{h}", i)
                        for c in range(2 * h, 2 * h + 2):
                            last = dve.tensor_scalar(half(tmp[h][:])[:, c % 2, :], eTf[:, c, :], w3_col[:, c:c + 1],
                                                     w2_col[:, c:c + 1], ALU.mult, ALU.add)
                        last.then_inc(f_ready["ew"], 1)
                if "ffn" in on:
                    wait(dve, out_ready, TT * l)
                    normalise("y", lambda t: y[:, t, :], lambda t: x2[:, t, :], l)
                if "xa" in on:
                    psum_lo("cT", cT, cT_hi, 2, m, i)
                    split_lo("ew", ewT, m)
                if "ffn" in on:
                    mix("xk", l)
                    split_lo("xk", xkT, l)
                if "att" in on:
                    scale_values(n, 0)
                if "xa" in on:
                    wait_filled(dve, "sim", i)
                    dve.tensor_reduce(neg_max[:], half(ps["T0"][:]), AX.X, ALU.max, negate=True)\
                        .then_inc(neg_max_ready, 1)
                if "att" in on:
                    add_values(n, 0)
                if "ffn" in on:
                    mix("xr", l)
                if "xa" in on:
                    wait_drained(dve, "sim", i)
                    dve.reciprocal(a_rsum[:], a_sum[:]).then_inc(a_rsum_ready, 1)
                    dve.wait_ge(e_w1_ready, TT * (m + 1))
                    dve.scalar_tensor_tensor(u[:], neg_max[:], -1.0, e_w1[:], ALU.mult, ALU.add).then_inc(u_ready, 1)
                    dve.wait_ge(a_rsum_ready, m + 1)
                    for t in range(TT):
                        dve.tensor_scalar(a[:, t, :], a[:, t, :], a_rsum[:, t:t + 1], None, ALU.mult)\
                            .then_inc(a_normed, 1)
                if "ffn" in on:
                    split_lo("xr", xrT, l)
                    wait_tmp(dve, "ka", i)
                    for h in range(2):
                        wait_drained(dve, f"k{h}", i)
                        dve.tensor_tensor(tmp[h][:], y[:, h, :], y[:, h, :], ALU.mult).then_inc(f_ready["ka"], 1)
                    split_lo("ka", kaT, l)
                if "att" in on:
                    attend(n, 1)
                if "pre" in on:
                    dve.wait_ge(x_loaded, 16 * (p + 1))
                    layernorm_stats("x", x_in, p)
                if "xa" in on:
                    dve.wait_ge(aT_hi, m + 1)
                    dve.tensor_tensor(aT[1], half(ps[BANK["aT"]][:]), aT[0].bitcast(F32), ALU.subtract)\
                        .then_inc(drained[BANK["aT"]], 1)
                if "ffn" in on:
                    gate(0)
                if "att" in on:
                    attend(n, 2)
                if "xa" in on:
                    wait_filled(dve, "ub", i)
                    dve.tensor_reduce(ub_neg_max[:], ps[BANK["ub"]][:, 0:S], AX.X, ALU.max, negate=True)\
                        .then_inc(ub_max_ready, 1)
                    wait_drained(dve, "ub", i)
                    dve.reciprocal(ub_rsum[:], ub_sum[:]).then_inc(ub_rsum_ready, 1)
                    wait_tmp(dve, "hc", i)
                    dve.wait_ge(ub_rsum_ready, m + 1)
                    for c in range(C):
                        dve.tensor_tensor_reduce(tmp[c // 2][:, (c % 2) * S:(c % 2 + 1) * S], eTf[:, c, :], batt,
                                                 ub_rsum[:], 0.0, ALU.mult, ALU.add, hc[:, c:c + 1])\
                            .then_inc(hc_ready, 1)
                if "ffn" in on:
                    gate(1)
                if "xa" in on:
                    wait_tmp(dve, "weff", i)
                    merge(0)
                    merge(1)
                    merged_lo(0)
                    merged_lo(1)
                    wait_tmp(dve, "eh", i)
                    for h in range(2):
                        bank = BANK[f"hq{h}"]
                        dve.wait_ge(hqT_hi, 2 * m + h + 1)
                        dve.tensor_tensor(hqT[1][:, 2 * h:2 * h + 2, :], half(ps[bank][:]),
                                          hqT[0][:, 2 * h:2 * h + 2, :].bitcast(F32), ALU.subtract)
                        dve.tensor_tensor(tmp[h][:], ps[bank][:], eTf[:, 2 * h:2 * h + 2, :].rearrange(
                            "p c s -> p (c s)"), ALU.mult).then_inc(drained[bank], 1)
                    split_lo("eh", ehT, m)
                if "att" in on:
                    attend(n, 3)
                if "xa" in on:
                    wait_tmp(dve, "weff_rest", i)
                    merge(2)
                    merge(3)
                    merged_lo(2)
                    merged_lo(3)
                if "pre" in on:
                    if "att" in on:
                        wait_filled(dve, "pv3", i)
                    normalise("x", lambda t: xn[:, t, 0:D], lambda t: x_in[:, t, :], p)
                if "att" in on:
                    dve.wait_ge(x1_ready, G * (n + 1))
                    layernorm_stats("e", x1, n)
                if "pre" in on:
                    psum_lo("xT", xT, xT_hi, 2, p, i)
                if "att" in on:
                    if "pre" in on:
                        dve.wait_ge(normed["x"], TT * (p + 1))
                    normalise("e", lambda t: e[:, t, :], lambda t: x1[:, t, :], n)
                    dve.wait_ge(normed["e"], TT * (n + 1))
                    wait_tmp(dve, "e_w1", i)
                    for t in range(TT):
                        dve.tensor_tensor_reduce(tmp[t][:], e[:, t, :], w1_row[:], 1.0, b_sim_col[:], ALU.mult,
                                                 ALU.add, e_w1[:, t:t + 1]).then_inc(e_w1_ready, 1)
                if "xa" in on:
                    wait(dve, out_stored, 16 * TT * m)
                    for t in range(TT):
                        wait_filled(dve, f"h{t}", i)
                        if t == 0:
                            dve.wait_ge(x1b_ready, m + 1)
                        dve.tensor_tensor(x2[:, t, :], ps[BANK[f"h{t}"]][:], x1b[:, t, :], ALU.add)\
                            .then_inc(drained[BANK[f"h{t}"]], 1)
                    wait_drained(dve, "h0", i)
                    wait_drained(dve, "h1", i)
                    layernorm_stats("y", x2, m)

            steps(dve, step)

        @block.tensor
        def _(pe):
            def transpose(dst, src, n=P):
                return pe.transpose(dst, src, ident[:])

            def product(dst, lhs, rhs, start, stop):
                last = None
                for n, (x, w) in enumerate(((0, 0), (0, 1), (1, 0))):
                    last = pe.matmul(dst, lhs[x], rhs[w], start=start and n == 0, stop=stop and n == 2)
                return last

            def claim(name, i):
                pe.wait_ge(drained[BANK[name]], fill_number(name, i) - 1)
                return ps[BANK[name]]

            def parts(pair, *index):
                return [t[index] for t in pair]

            ALL = slice(None)

            pe.wait_ge(consts_ready, 5)
            for n, name in enumerate(("wkT", "wrT", "wvT")):
                wait_staged(pe, 2 * n)
                wait_staged(pe, 2 * n + 1)
                for kc in range(C):
                    bank = BANKS[kc]
                    wait(pe, drained[bank], n)
                    for dc in range(C):
                        src = stage[(2 * n + dc // 2) % len(stage)][:, dc % 2, kc * P:(kc + 1) * P]
                        last = transpose(ps[bank][:, dc * P:(dc + 1) * P], src)
                    last.then_inc(filled[bank], 1)
                pe.wait_ge(drained[BANKS[-1]], n + 1)
                pe.sem_inc(w_turned, 1)

            def turn(name, src, i):
                for h in range(2):
                    dst = claim(f"{name}{h}", i)
                    for c in range(2 * h, 2 * h + 2):
                        for t in range(TT):
                            at = (c % 2) * S + t * P
                            last = transpose(dst[:, at:at + P], src(t, c))
                    last.then_inc(filled[BANK[f"{name}{h}"]], 1)

            def scores(n, g):
                if g:
                    pe.wait_ge(probs_ready, G * n + g)
                else:
                    wait(pe, probs_ready, G * n)
                for k in range(TT):
                    q = slice(k * P, S)
                    at = slice(k * S, k * S + S - k * P)
                    for nth, (lhs, rhs) in enumerate(((0, 0), (0, 1), (1, 0))):
                        for r in range(R):
                            rows = slice(r * HD, (r + 1) * HD)
                            last = pe.matmul(ps_scores[:, r, at], xT[lhs][rows, g, k * P:(k + 1) * P],
                                             xT[rhs][rows, g, q], start=nth == 0, stop=nth == 2)
                last.then_inc(scores_ready, 1)

            def head(k, h):
                v = xn[:, k, h * HD:(h + 1) * HD]
                return bass.AP(tensor=v.tensor, offset=v.offset, ap=[list(v.ap[0]), [D - h * HD, 2], [1, HD]])

            def values(n, g):
                name = f"pv{g}"
                dst = claim(name, n)
                pe.wait_ge(probs_masked, G * n + g + 1)
                for t in range(TT):
                    for r in range(R):
                        at = (t * R + r) * 2 * HD
                        for k in range(t + 1):
                            cols = slice((k + t) * P, (k + t + 1) * P)
                            last = pe.matmul(dst[:, at:at + 2 * HD], probs[:, r, cols], head(k, g * R + r),
                                             start=k == 0, stop=k == t)
                last.then_inc(filled[BANK[name]], 1)

            def tokens_by(name, i, pairs, t):
                dst = claim(name, i)
                todo = [(x, w, c) for x, w in pairs for c in range(C)]
                for n, (x, w, c) in enumerate(todo):
                    last = product(dst[:], parts(x, ALL, c, slice(t * P, (t + 1) * P)), parts(w, ALL, c, ALL),
                                   n == 0, n == len(todo) - 1)
                last.then_inc(filled[BANK[name]], 1)

            def step(i, on):
                p, n, m, l = i + 1, i, i - 1, i - 2

                def weighted(name, source, weights, t):
                    tokens_by(f"{name}{t}", i, [(source, wT[weights])], t)

                def features(t, lhs, rhs, start, stop):
                    for c in range(C):
                        last = product(ps[BANK[f"h{t}"]][:], parts(lhs, ALL, c, slice(t * P, (t + 1) * P)), rhs(c),
                                       start and c == 0, stop and c == C - 1)
                    if stop:
                        last.then_inc(filled[BANK[f"h{t}"]], 1)

                if "xa" in on:
                    pe.wait_ge(normed["e"], TT * (m + 1))
                    turn("eT", lambda t, c: e[:, t, c * P:(c + 1) * P], i)
                if "att" in on:
                    wait_drained(pe, "xT1", i - 1)
                    wait_drained(pe, "xT0", i - 1)
                    scores(n, 0)
                if "xa" in on:
                    pe.wait_ge(ctx_loaded, 16 * (m + 1))
                    turn("cT", lambda t, c: ctx_sb[:, t, c * P:(c + 1) * P], i)
                if "ffn" in on:
                    pe.wait_ge(normed["y"], TT * (l + 1))
                    turn("yT", lambda t, c: y[:, t, c * P:(c + 1) * P], i)
                if "att" in on:
                    scores(n, 1)
                    values(n, 0)
                if "xa" in on:
                    pe.wait_ge(split["ew"], 2 * (m + 1))
                    wait_drained(pe, "cT1", i)
                    dst = claim("sim", i)
                    for t in range(TT):
                        for c in range(C):
                            last = product(dst[:, t * S:(t + 1) * S], parts(ewT, ALL, c, slice(t * P, (t + 1) * P)),
                                           parts(cT, ALL, c, ALL), c == 0, c == C - 1)
                    last.then_inc(filled[BANK["sim"]], 1)
                if "ffn" in on:
                    pe.wait_ge(split["xk"], 2 * (l + 1))
                    for h in range(2):
                        dst = claim(f"k{h}", i)
                        for d in range(2 * h, 2 * h + 2):
                            for c in range(C):
                                last = product(dst[:, (d % 2) * S:(d % 2 + 1) * S],
                                               parts(wT["wkT"], ALL, c, slice(d * P, (d + 1) * P)),
                                               parts(xkT, ALL, c, ALL), c == 0, c == C - 1)
                        last.then_inc(filled[BANK[f"k{h}"]], 1)
                if "att" in on:
                    values(n, 1)
                    scores(n, 2)
                if "ffn" in on:
                    pe.wait_ge(split["xr"], 2 * (l + 1))
                    weighted("r", xrT, "wrT", 0)
                if "xa" in on:
                    pe.wait_ge(a_normed, TT * (m + 1))
                    dst = claim("aT", i)
                    for j in range(TT):
                        for t in range(TT):
                            last = transpose(dst[:, j * S + t * P:j * S + (t + 1) * P], a[:, t, j * P:(j + 1) * P])
                    last.then_inc(filled[BANK["aT"]], 1)
                if "ffn" in on:
                    pe.wait_ge(split["ka"], 2 * (l + 1))
                    weighted("v", kaT, "wvT", 0)
                    weighted("r", xrT, "wrT", 1)
                if "att" in on:
                    values(n, 2)
                    scores(n, 3)
                if "xa" in on:
                    pe.wait_ge(u_ready, m + 1)
                    dst = claim("ub", i)
                    for t in range(TT):
                        last = pe.matmul(dst[:, t * P:(t + 1) * P], u[:, t:t + 1].to_broadcast([P, P]), ident[:],
                                         start=True, stop=True)
                    last.then_inc(filled[BANK["ub"]], 1)
                if "ffn" in on:
                    weighted("v", kaT, "wvT", 1)
                if "xa" in on:
                    pe.wait_ge(ctx_split, m + 1)
                    wait_drained(pe, "aT", i)
                    for h in range(2):
                        dst = claim(f"hq{h}", i)
                        for c in range(2 * h, 2 * h + 2):
                            for j in range(TT):
                                last = product(dst[:, (c % 2) * S:(c % 2 + 1) * S],
                                               parts(c_rows, ALL, j, slice(c * P, (c + 1) * P)),
                                               parts(aT, ALL, j, ALL), j == 0, j == TT - 1)
                        last.then_inc(filled[BANK[f"hq{h}"]], 1)
                if "att" in on:
                    values(n, 3)
                if "xa" in on:
                    wait_drained(pe, "hq0", i)
                    wait_drained(pe, "hq1", i)
                    for t in range(TT):
                        features(t, hqT, lambda c: parts(wqv2, ALL, c, ALL), True, False)
                    pe.wait_ge(split["eh"], 2 * (m + 1))
                    for t in range(TT):
                        features(t, ehT, lambda c: parts(wqv3, ALL, c, ALL), False, False)
                if "pre" in on:
                    pe.wait_ge(normed["x"], TT * (p + 1))
                    turn("xT", lambda t, c: xn[:, t, c * P:(c + 1) * P], i)
                if "xa" in on:
                    pe.wait_ge(eT_split, 2 * (m + 1))
                    pe.wait_ge(split["weff"], C * (m + 1))
                    for t in range(TT):
                        features(t, eT, lambda c: parts(weff[c], ALL, 0, ALL), False, True)

            steps(pe, step)


_INS = ["x", "ctx_1024", "L0_xattn_w_sim", "L0_xattn_b_sim", "L0_xattn_W_qv", "L0_xattn_b_qv", "L0_ffn_W_r",
        "L0_ffn_W_k", "L0_ffn_W_v", "L0_ffn_mu_r", "L0_ffn_mu_k"]


def kernel(**inputs):
    import numpy as np
    import concourse.bacc as bacc
    from concourse.bass_utils import run_bass_kernel_spmd as run

    nc = bacc.Bacc("TRN2", target_bir_lowering=False, num_devices=1)
    arrays, args = {}, []
    for name in _INS:
        arrays[f"in_{name}"] = np.ascontiguousarray(inputs[name])
        args.append(nc.dram_tensor(f"in_{name}", arrays[f"in_{name}"].shape, F32, kind="ExternalInput").ap())
    args.append(nc.dram_tensor("out", (B, S, D), F32, kind="ExternalOutput").ap())
    build(nc, *args)
    return run(nc, [arrays], core_ids=[0]).results[0]["out"]
```

```python
from contextlib import ExitStack

import concourse.bass as bass
from concourse import mybir

ACT = mybir.ActivationFunctionType
ALU = mybir.AluOpType
AX = mybir.AxisListType
F32 = mybir.dt.float32
F32R = mybir.dt.float32r

P = 128
B, S, D = 32, 256, 512
H = 16
HD = D // H
TT = S // P
C = D // P
G = C
R = H // G
EPS = 1e-5
SCALE = HD ** -0.5
SHIFT = D * SCALE / 2

MERGE_ORDER = [2, 3, 0, 1]

LATE = {"pre": -1, "att": 0, "xa": 1, "ffn": 2}
FILLS = {
    "T0": [("eT0", "xa"), ("yT0", "ffn"), ("sim", "xa"), ("aT", "xa"), ("ub", "xa"),
           ("xT0", "pre")],
    "T1": [("eT1", "xa"), ("yT1", "ffn"), ("pv0", "att"), ("pv1", "att"),
           ("pv2", "att"), ("pv3", "att"), ("xT1", "pre")],
    "D0": [("cT0", "xa"), ("k0", "ffn"), ("r0", "ffn"), ("r1", "ffn"), ("hq0", "xa"), ("h0", "xa")],
    "D1": [("cT1", "xa"), ("k1", "ffn"), ("v0", "ffn"), ("v1", "ffn"), ("hq1", "xa"), ("h1", "xa")],
}
BANK = {name: bank for bank, fills in FILLS.items() for name, _ in fills}
BANKS = list(FILLS)
TMP_USES = [("ew", "xa", "ew", 2, 2), ("xk", "ffn", "xk", 2, 2), ("xr", "ffn", "xr", 2, 2), ("ka", "ffn", "ka", 2, 2), ("hc", "xa", "hc", C, C),
            ("eh", "xa", "eh", 2, 2), ("weff", "xa", "weff", C, C), ("e_w1", "att", "e_w1", TT, TT)]
SETUP_FILLS = 3


def fill_number(name, i):
    fills = FILLS[BANK[name]]
    at = [f for f, _ in fills].index(name)
    through = [LATE[stage] - (n <= at) for n, (_, stage) in enumerate(fills)]
    if isinstance(i, int):
        return SETUP_FILLS + sum(min(max(i - late, 0), B) for late in through)
    return i * len(fills) + (SETUP_FILLS - sum(through))


def build(nc, x, ctx_in, w_sim, b_sim, w_qv, b_qv, w_r, w_k, w_v, mu_r, mu_k, out):
    with ExitStack() as stack:
        def sb(name, shape, dt=F32):
            return stack.enter_context(nc.sbuf_tensor(name, shape, dt))

        def sem(name):
            return stack.enter_context(nc.semaphore(name))

        ident = sb("ident", [P, P])
        neg_half = sb("neg_half", [P, TT])
        neg_shift = sb("neg_shift", [P, 1])
        w1_row = sb("w1_row", [P, D])
        b_sim_col = sb("b_sim_col", [P, 1])
        b_row = sb("b_row", [P, D])
        w2_col = sb("w2_col", [P, C])
        w3_col = sb("w3_col", [P, C])
        mu = {"xk": sb("mu_k_col", [P, C]), "xr": sb("mu_r_col", [P, C])}
        wqv1 = sb("wqv1", [P, C, D])
        wqv4 = sb("wqv4", [P, C, D])
        wqv2 = [sb(f"wqv2_{h}", [P, C, D], F32R) for h in ("hi", "lo")]
        wqv3 = [sb(f"wqv3_{h}", [P, C, D], F32R) for h in ("hi", "lo")]
        wT = {n: [sb(f"{n}_{h}", [P, C, D], F32R) for h in ("hi", "lo")] for n in ("wrT", "wkT", "wvT")}

        ctx_sb = sb("ctx_sb", [P, TT, D])
        xn = sb("xn", [P, TT, D + HD])
        x1 = sb("x1", [P, TT, D])
        x1b = sb("x1b", [P, TT, D])
        e = sb("e", [P, TT, D])
        x2 = sb("x2", [P, TT, D])
        y = sb("y", [P, TT, D])
        x_in = e
        a = sb("a", [P, TT, S])
        probs = sb("probs", [P, R, 3 * P])
        pv_scaled = sb("pv_scaled", [P, TT, R, HD])
        tmp = [sb(f"tmp{n}", [P, D]) for n in range(2)]
        eTf = sb("eTf", [P, C, S])
        eT = [sb(f"eT_{h}", [P, C, S], F32R) for h in ("hi", "lo")]
        xT = [sb(f"xT_{h}", [P, C, S], F32R) for h in ("hi", "lo")]
        yT = sb("yT", [P, C, S + 1])
        area_c = sb("area_c", [P, 2 * C * S], F32R)
        area_k = sb("area_k", [P, 2 * C * S], F32R)
        area_e = sb("area_e", [P, 2 * C * S], F32R)
        area_x = sb("area_x", [P, 2 * C * S], F32R)
        area_m = sb("area_m", [P, 2 * C * S], F32R)

        def pair(area, n, width, base=0, step=C * S):
            return [area[:, base + h * step:base + h * step + n * width].rearrange("p (c s) -> p c s", c=n)
                    for h in range(2)]

        cT, kaT, ewT, ehT = (pair(t, C, S) for t in (area_c, area_k, area_e, area_e))
        xrT, hqT, xkT = (pair(t, C, S) for t in (area_x, area_x, area_m))
        c_rows = pair(area_m, TT, D)
        aT = pair(area_c, TT, S, step=TT * S)
        weff = [pair((area_c, area_k)[c // 2], 1, D, base=(c % 2) * D) for c in range(C)]

        stats = {n: sb(f"stats_{n}", [P, TT, 6]) for n in "xey"}
        moments = {n: sb(f"moments_{n}", [P, TT, 2]) for n in "xey"}
        var = {n: sb(f"var_{n}", [P, TT]) for n in "xey"}
        rstd = {n: sb(f"rstd_{n}", [P, TT]) for n in "xey"}
        r_den = sb("r_den", [P, G, TT, R])
        e_w1 = sb("e_w1", [P, TT])
        neg_max = sb("neg_max", [P, TT])
        a_sum = sb("a_sum", [P, TT])
        a_rsum = sb("a_rsum", [P, TT])
        u = sb("u", [P, TT])
        ub_neg_max = sb("ub_neg_max", [P, 1])
        ub_sum = sb("ub_sum", [P, 1])
        ub_rsum = sb("ub_rsum", [P, 1])
        batt = a[:, 0, :]
        hc = sb("hc", [P, C])

        ps = {n: stack.enter_context(nc.psum_tensor(n, [P, D], F32)) for n in BANKS}
        ps_scores = stack.enter_context(nc.psum_tensor("ps_scores", [P, R, D], F32))

        filled = {n: sem(f"filled_{n}") for n in BANKS}
        drained = {n: sem(f"drained_{n}") for n in BANKS}

        x_loaded, ctx_loaded, x1_loaded, out_stored = map(sem, ("x_loaded", "ctx_loaded", "x1_loaded", "out_stored"))
        small_loaded, w_turned, w_split, wqv_loaded = map(sem, ("small_loaded", "w_turned", "w_split", "wqv_loaded"))
        stage_loaded = [sem(f"stage_loaded_{n}") for n in range(4)]
        w_hi, consts_ready, ident_zero = map(sem, ("w_hi", "consts_ready", "ident_zero"))
        stats_done = {n: sem(f"stats_done_{n}") for n in "xey"}
        moments_done = {n: sem(f"moments_done_{n}") for n in "xey"}
        var_done = {n: sem(f"var_done_{n}") for n in "xey"}
        rstd_done = {n: sem(f"rstd_done_{n}") for n in "xey"}
        normed = {n: sem(f"normed_{n}") for n in "xey"}
        scores_ready, probs_ready, probs_masked = map(sem, ("scores_ready", "probs_ready", "probs_masked"))
        den_ready, pv_scaled_ready, x1_ready, x1b_ready = map(
            sem, ("den_ready", "pv_scaled_ready", "x1_ready", "x1b_ready"))
        eT_hi, eT_split, cT_hi, xT_hi, aT_hi, hqT_hi = map(
            sem, ("eT_hi", "eT_split", "cT_hi", "xT_hi", "aT_hi", "hqT_hi"))
        KINDS = ("ew", "xk", "xr", "ka", "eh", "weff")
        f_ready = {n: sem(f"{n}_f") for n in KINDS}
        hi_ready = {n: sem(f"{n}_hi") for n in KINDS}
        split = {n: sem(f"{n}_split") for n in KINDS}
        steps_ready = sem("steps_ready")
        ctx_hi, ctx_split = sem("ctx_hi"), sem("ctx_split")
        pool_passed, dve_passed, sp_passed = map(sem, ("pool_passed", "dve_passed", "sp_passed"))
        out_ready = sem("out_ready")
        neg_max_ready, a_exp, a_rsum_ready, a_normed, e_w1_ready, u_ready = map(
            sem, ("neg_max_ready", "a_exp", "a_rsum_ready", "a_normed", "e_w1_ready", "u_ready"))
        ub_max_ready, batt_ready, ub_rsum_ready, hc_ready = map(
            sem, ("ub_max_ready", "batt_ready", "ub_rsum_ready", "hc_ready"))

        def wait(eng, semaphore, value):
            if not isinstance(value, int) or value > 0:
                eng.wait_ge(semaphore, value)

        def wait_filled(eng, name, i):
            eng.wait_ge(filled[BANK[name]], fill_number(name, i))

        def wait_drained(eng, name, i):
            eng.wait_ge(drained[BANK[name]], fill_number(name, i))

        def stages(i):
            return {n for n, late in LATE.items() if 0 <= i - late < B}

        def wait_tmp(eng, kind, i):
            tmp_used = {**split, "hc": hc_ready, "e_w1": e_w1_ready}
            at = [use[0] for use in TMP_USES].index(kind)
            for n in range(at - 1, at - 1 - len(TMP_USES), -1):
                _, stage_name, count, upto, per = TMP_USES[n]
                j = i - (n < 0)
                if not isinstance(i, int) or stage_name in stages(j):
                    eng.wait_ge(tmp_used[count], per * (j - LATE[stage_name]) + upto)
                    return

        def half(bank_ap):
            return bank_ap.rearrange("p (c s) -> p c s", c=2)

        def steps(eng, step):
            first = max(LATE.values())
            last = B - 1 + min(LATE.values())
            for i in range(min(LATE.values()), first):
                step(i, stages(i))
            with eng.Fori(first, last + 1) as i:
                step(i, set(LATE))
            for i in range(last + 1, B + max(LATE.values())):
                step(i, stages(i))

        stage = [x1, x1b, e, x2]
        staged = [(n, h) for n in ("wkT", "wrT", "wvT", "wqv2", "wqv3") for h in range(2)]

        def wait_staged(eng, n):
            eng.wait_ge(stage_loaded[n % len(stage)], 16 * (n // len(stage) + 1))

        def wait_stage_free(eng):
            eng.wait_ge(w_turned, 3)
            eng.wait_ge(w_split, len(staged) - 6)

        block = stack.enter_context(nc.Block())

        @block.sync
        def _(sp):
            xv = x.rearrange("b (t p) d -> b p t d", p=P)
            cv = ctx_in.rearrange("b (t p) d -> b p t d", p=P)
            ov = out.rearrange("b (t p) d -> b p t d", p=P)
            wqv = w_qv.rearrange("(q h c p) d -> q h p c d", q=4, h=2, p=P)
            dram = {"wkT": w_k, "wrT": w_r, "wvT": w_v}
            for n, (name, h) in enumerate(staged):
                if n >= len(stage):
                    sp.wait_ge(w_turned, (n - len(stage)) // 2 + 1)
                src = wqv[int(name[-1]) - 1, h] if name in ("wqv2", "wqv3") else \
                    dram[name].rearrange("(h c p) d -> h p c d", h=2, p=P)[h]
                sp.dma_start(stage[n % len(stage)][:], src).then_inc(stage_loaded[n % len(stage)], 16)
                if n == 3:
                    sp.dma_start(ctx_sb[:], cv[0]).then_inc(ctx_loaded, 16)
            for h in range(2):
                sp.dma_start(wqv1[:, 2 * h:2 * h + 2, :], wqv[0, h]).then_inc(wqv_loaded, 16)
                sp.dma_start(wqv4[:, 2 * h:2 * h + 2, :], wqv[3, h]).then_inc(wqv_loaded, 16)

            def step(i, on):
                p, n, m, l = i + 1, i, i - 1, i - 2
                if "pre" in on:
                    if "xa" in on:
                        wait_filled(sp, "eT1", i)
                        sp.sem_inc(sp_passed, 1)
                        sp.wait_ge(e_w1_ready, TT * (m + 1))
                    elif p:
                        sp.wait_ge(normed["x"], TT * p)
                    else:
                        wait_stage_free(sp)
                    sp.dma_start(x_in[:], xv[p]).then_inc(x_loaded, 16)
                if "att" in on:
                    if isinstance(n, int) and n == 0:
                        wait_stage_free(sp)
                    wait(sp, normed["e"], TT * n)
                    wait(sp, x1b_ready, n)
                    sp.dma_start(x1[:], xv[n]).then_inc(x1_loaded, 16)
                if "xa" in on and not (isinstance(m, int) and m == B - 1):
                    sp.wait_ge(ctx_split, m + 1)
                    sp.dma_start(ctx_sb[:], cv[m + 1]).then_inc(ctx_loaded, 16)
                if "ffn" in on:
                    for t in range(TT):
                        sp.wait_ge(out_ready, TT * l + t + 1)
                        sp.dma_start(ov[l][:, t], x2[:, t, :]).then_inc(out_stored, 16)

            steps(sp, step)
            sp.wait_ge(out_stored, 16 * TT * B)

        @block.gpsimd
        def _(pool):
            pool.memset(ident[:], 0.0).then_inc(ident_zero, 1)
            pool.memset(neg_half[:], -0.5).then_inc(consts_ready, 1)
            pool.memset(neg_shift[:], -SHIFT).then_inc(consts_ready, 1)
            pool.memset(xn[:, :, D:], 1.0).then_inc(consts_ready, 1)
            pool.memset(yT[:, :, 0:1], 0.0).then_inc(consts_ready, 1)
            pool.wait_ge(ident_zero, 1)
            pool.affine_select(out=ident[:], in_=ident[:], compare_op=ALU.not_equal, fill=1.0, base=0,
                               pattern=[[-1, P]], channel_multiplier=1).then_inc(consts_ready, 1)
            pool.dma_start(w2_col[:], w_sim[D:2 * D].rearrange("(c p) -> p c", p=P),
                           allow_slow_non_contiguous=True).then_inc(small_loaded, 16)
            pool.dma_start(w3_col[:], w_sim[2 * D:3 * D].rearrange("(c p) -> p c", p=P),
                           allow_slow_non_contiguous=True).then_inc(small_loaded, 16)
            pool.dma_start(mu["xr"][:], mu_r.rearrange("(c p) -> p c", p=P),
                           allow_slow_non_contiguous=True).then_inc(small_loaded, 16)
            pool.dma_start(mu["xk"][:], mu_k.rearrange("(c p) -> p c", p=P),
                           allow_slow_non_contiguous=True).then_inc(small_loaded, 16)
            pool.dma_start(w1_row[:], w_sim[0:D].partition_broadcast(P)).then_inc(small_loaded, 16)
            pool.dma_start(b_row[:], b_qv.partition_broadcast(P)).then_inc(small_loaded, 16)
            pool.dma_start(b_sim_col[:], b_sim.partition_broadcast(P)).then_inc(small_loaded, 16)
            pool.wait_ge(small_loaded, 7 * 16)
            pool.wait_ge(consts_ready, 5)

            def root(n, b):
                pool.wait_ge(var_done[n], b + 1)
                pool.tensor_tensor(rstd[n][:], var[n][:], neg_half[:], ALU.pow).then_inc(rstd_done[n], 1)

            def mask(n, g):
                pool.wait_ge(probs_ready, G * n + g + 1)
                pool.sem_inc(pool_passed, 1)
                for k in range(TT):
                    diag = probs[:, :, 2 * k * P:(2 * k + 1) * P]
                    last = pool.affine_select(out=diag, in_=diag, compare_op=ALU.is_ge, fill=0.0, base=0,
                                              pattern=[[0, R], [1, P]], channel_multiplier=-1)
                last.then_inc(probs_masked, 1)

            def add_out(i, l, t):
                wait_drained(pool, f"v{t}", i)
                pool.tensor_tensor(x2[:, t, :], x2[:, t, :], y[:, t, :], ALU.add).then_inc(out_ready, 1)

            def step(i, on):
                p, n, m, l = i + 1, i, i - 1, i - 2
                if "att" in on:
                    mask(n, 0)
                if "ffn" in on:
                    root("y", l)
                if "xa" in on:
                    pool.wait_ge(x1_ready, G * (m + 1))
                    if isinstance(m, int) and m == 0:
                        wait_stage_free(pool)
                    else:
                        wait_drained(pool, "h0", i - 1)
                        wait_drained(pool, "h1", i - 1)
                    for t in range(TT):
                        last = pool.tensor_tensor(x1b[:, t, :], x1[:, t, :], b_row[:], ALU.add)
                    last.then_inc(x1b_ready, 1)
                if "att" in on:
                    mask(n, 1)
                if "xa" in on:
                    for h in range(2):
                        pool.wait_ge(eT_hi, 2 * m + h + 1)
                        pool.tensor_tensor(eT[1][:, 2 * h:2 * h + 2, :], eTf[:, 2 * h:2 * h + 2, :],
                                           eT[0][:, 2 * h:2 * h + 2, :].bitcast(F32), ALU.subtract)\
                            .then_inc(eT_split, 1)
                    pool.wait_ge(ctx_loaded, 16 * (m + 1))
                    wait_filled(pool, "cT1", i)
                    if "ffn" in on:
                        wait_filled(pool, "k1", i)
                    pool.sem_inc(pool_passed, 1)
                    for t in range(TT):
                        last = pool.tensor_scalar(c_rows[0][:, t, :], ctx_sb[:, t, :], 1.0, 0.0, ALU.mult, ALU.add)
                    last.then_inc(ctx_hi, 1)
                    pool.wait_ge(ctx_hi, m + 1)
                    for t in range(TT):
                        last = pool.tensor_tensor(c_rows[1][:, t, :], ctx_sb[:, t, :],
                                                  c_rows[0][:, t, :].bitcast(F32), ALU.subtract)
                    last.then_inc(ctx_split, 1)
                if "att" in on:
                    mask(n, 2)
                if "pre" in on:
                    root("x", p)
                if "ffn" in on:
                    add_out(i, l, 0)
                if "att" in on:
                    mask(n, 3)
                if "ffn" in on:
                    add_out(i, l, 1)
                if "att" in on:
                    root("e", n)

            steps(pool, step)

        @block.scalar
        def _(act):
            def copy(dst, src):
                return act.activation(dst, src, ACT.Copy)

            done = 0
            for n, name in enumerate(("wkT", "wrT", "wvT")):
                for kc in range(C):
                    bank = BANKS[kc]
                    act.wait_ge(filled[bank], n + 1)
                    act.activation(wT[name][0][:, kc, :], ps[bank][:], ACT.Copy,
                                   scale=0.5 if name == "wvT" else 1.0).then_inc(w_hi, 1)
            for n in range(6, len(staged)):
                name, h = staged[n]
                dst = (wqv2 if name == "wqv2" else wqv3)[0]
                wait_staged(act, n)
                copy(dst[:, 2 * h:2 * h + 2, :], stage[n % len(stage)][:]).then_inc(w_hi, 1)
            act.wait_ge(consts_ready, 5)
            act.wait_ge(small_loaded, 7 * 16)

            def exp_scores(n, g):
                act.wait_ge(scores_ready, G * n + g + 1)
                if g:
                    wait_filled(act, f"pv{g - 1}", n)
                elif not isinstance(n, int) or n > 0:
                    wait_filled(act, f"pv{G - 1}", n - 1)
                act.activation(probs[:], ps_scores[:, :, 0:3 * P], ACT.Exp, bias=neg_shift[:], scale=SCALE)\
                    .then_inc(probs_ready, 1)

            def split_hi(kind, dst, b):
                for h in range(2):
                    act.wait_ge(f_ready[kind], 2 * b + h + 1)
                    copy(dst[0][:, 2 * h:2 * h + 2, :], half(tmp[h][:])).then_inc(hi_ready[kind], 1)

            def psum_hi(name, dst, done, i):
                for h in range(2):
                    wait_filled(act, f"{name}{h}", i)
                    copy(dst[0][:, 2 * h:2 * h + 2, :], half(ps[BANK[f"{name}{h}"]][:])).then_inc(done, 1)

            def step(i, on):
                p, n, m, l = i + 1, i, i - 1, i - 2
                def merged_hi(at):
                    act.wait_ge(f_ready["weff"], C * m + at + 1)
                    copy(weff[MERGE_ORDER[at]][0][:, 0, :], tmp[at % 2][:]).then_inc(hi_ready["weff"], 1)

                def tanh(t):
                    wait_filled(act, f"r{t}", i)
                    act.activation(y[:, t, :], ps[BANK[f"r{t}"]][:], ACT.Tanh, scale=0.5)\
                        .then_inc(drained[BANK[f"r{t}"]], 1)

                if "att" in on:
                    exp_scores(n, 0)
                if "xa" in on:
                    for h in range(2):
                        wait_filled(act, f"eT{h}", i)
                        copy(eTf[:, 2 * h:2 * h + 2, :], half(ps[BANK[f"eT{h}"]][:]))\
                            .then_inc(drained[BANK[f"eT{h}"]], 1)
                if "xa" in on:
                    psum_hi("cT", cT, cT_hi, i)
                    wait_tmp(act, "ew", i)
                    wait_drained(act, "eT1", i)
                    for h in range(2):
                        for c in range(2 * h, 2 * h + 2):
                            last = act.activation(half(tmp[h][:])[:, c % 2, :], eTf[:, c, :], ACT.Identity,
                                                  bias=w2_col[:, c:c + 1], scale=w3_col[:, c:c + 1])
                        last.then_inc(f_ready["ew"], 1)
                if "ffn" in on:
                    for h in range(2):
                        wait_filled(act, f"yT{h}", i)
                        copy(yT[:, 2 * h:2 * h + 2, 1:], half(ps[BANK[f"yT{h}"]][:]))\
                            .then_inc(drained[BANK[f"yT{h}"]], 1)
                if "xa" in on:
                    split_hi("ew", ewT, m)
                if "ffn" in on:
                    split_hi("xk", xkT, l)
                if "att" in on:
                    exp_scores(n, 1)
                if "xa" in on:
                    wait_filled(act, "sim", i)
                    act.wait_ge(neg_max_ready, m + 1)
                    for t in range(TT):
                        last = act.activation(a[:, t, :], ps["T0"][:, t * S:(t + 1) * S], ACT.Exp,
                                              bias=neg_max[:, t:t + 1], accum_out=a_sum[:, t:t + 1])
                        last.then_inc(a_exp if t == 0 else drained[BANK["sim"]], 1)
                    wait_drained(act, "eT1", i)
                    for h in range(2):
                        copy(eT[0][:, 2 * h:2 * h + 2, :], eTf[:, 2 * h:2 * h + 2, :]).then_inc(eT_hi, 1)
                if "ffn" in on:
                    split_hi("xr", xrT, l)
                    for h in range(2):
                        wait_filled(act, f"k{h}", i)
                        act.activation(y[:, h, :], ps[BANK[f"k{h}"]][:], ACT.Relu).then_inc(drained[BANK[f"k{h}"]], 1)
                    split_hi("ka", kaT, l)
                if "att" in on:
                    exp_scores(n, 2)
                if "xa" in on:
                    wait_filled(act, "aT", i)
                    copy(aT[0], half(ps[BANK["aT"]][:])).then_inc(aT_hi, 1)
                if "ffn" in on:
                    tanh(0)
                if "xa" in on:
                    act.wait_ge(ub_max_ready, m + 1)
                    act.activation(batt, ps[BANK["ub"]][:, 0:S], ACT.Exp, bias=ub_neg_max[:],
                                   accum_out=ub_sum[:]).then_inc(drained[BANK["ub"]], 1)
                if "ffn" in on:
                    tanh(1)
                if "att" in on:
                    exp_scores(n, 3)
                if "xa" in on:
                    psum_hi("hq", hqT, hqT_hi, i)
                    for h in range(2):
                        wait_drained(act, f"hq{h}", i)
                        copy(ehT[0][:, 2 * h:2 * h + 2, :], half(tmp[h][:])).then_inc(hi_ready["eh"], 1)
                    for at in range(C):
                        merged_hi(at)
                if "pre" in on:
                    psum_hi("xT", xT, xT_hi, i)

            steps(act, step)

        @block.vector
        def _(dve):
            n_hi = 0
            for n, name in enumerate(("wkT", "wrT", "wvT")):
                for kc in range(C):
                    bank = BANKS[kc]
                    n_hi += 1
                    dve.wait_ge(w_hi, n_hi)
                    dve.scalar_tensor_tensor(wT[name][1][:, kc, :], ps[bank][:], 0.5 if name == "wvT" else 1.0,
                                             wT[name][0][:, kc, :].bitcast(F32), ALU.mult, ALU.subtract)\
                        .then_inc(drained[bank], 1)
            for n in range(6, len(staged)):
                name, h = staged[n]
                dst = wqv2 if name == "wqv2" else wqv3
                n_hi += 1
                dve.wait_ge(w_hi, n_hi)
                dve.tensor_tensor(dst[1][:, 2 * h:2 * h + 2, :], stage[n % len(stage)][:],
                                  dst[0][:, 2 * h:2 * h + 2, :].bitcast(F32), ALU.subtract).then_inc(w_split, 1)
            dve.wait_ge(small_loaded, 7 * 16)
            dve.wait_ge(wqv_loaded, 4 * 16)
            wait_stage_free(dve)

            def psum_lo(name, dst, done, per, b, i):
                for h in range(2):
                    bank = BANK[f"{name}{h}"]
                    dve.wait_ge(done, per * b + h + 1)
                    dve.tensor_tensor(dst[1][:, 2 * h:2 * h + 2, :], half(ps[bank][:]),
                                      dst[0][:, 2 * h:2 * h + 2, :].bitcast(F32), ALU.subtract)\
                        .then_inc(drained[bank], 1)

            def split_lo(kind, dst, b):
                for h in range(2):
                    dve.wait_ge(hi_ready[kind], 2 * b + h + 1)
                    dve.tensor_tensor(dst[1][:, 2 * h:2 * h + 2, :], half(tmp[h][:]),
                                      dst[0][:, 2 * h:2 * h + 2, :].bitcast(F32), ALU.subtract)\
                        .then_inc(split[kind], 1)

            def layernorm_stats(n, src, b):
                for t in range(TT):
                    dve.bn_stats(stats[n][:, t, :], src[:, t, :]).then_inc(stats_done[n], 1)
                layernorm_moments(n, b)

            def layernorm_moments(n, b):
                dve.wait_ge(stats_done[n], TT * (b + 1))
                dve.sem_inc(dve_passed, 1)
                for t in range(TT):
                    dve.bn_aggr(moments[n][:, t, :], stats[n][:, t, :]).then_inc(moments_done[n], 1)
                dve.wait_ge(moments_done[n], TT * (b + 1))
                dve.tensor_scalar(var[n][:], moments[n][:, :, 1], EPS, None, ALU.add).then_inc(var_done[n], 1)

            def normalise(n, dst, src, b):
                dve.wait_ge(rstd_done[n], b + 1)
                for t in range(TT):
                    dve.tensor_scalar(dst(t), src(t), moments[n][:, t, 0:1], rstd[n][:, t:t + 1],
                                      ALU.subtract, ALU.mult).then_inc(normed[n], 1)

            def token_steps(b):
                for h in range(2):
                    dve.tensor_tensor(half(y[:, h, :]), yT[:, 2 * h:2 * h + 2, 1:], yT[:, 2 * h:2 * h + 2, 0:S],
                                      ALU.subtract).then_inc(steps_ready, 1)

            def mix(kind, b):
                for h in range(2):
                    dve.wait_ge(steps_ready, 2 * b + h + 1)
                    for c in range(2 * h, 2 * h + 2):
                        last = dve.scalar_tensor_tensor(half(tmp[h][:])[:, c % 2, :], half(y[:, h, :])[:, c % 2, :],
                                                        mu[kind][:, c:c + 1], yT[:, c, 0:S], ALU.mult, ALU.add)
                    last.then_inc(f_ready[kind], 1)

            def scale_values(n, g):
                wait_filled(dve, f"pv{g}", n)
                o = ps["T1"][:].rearrange("p (t r d) -> p t r d", t=TT, r=R)
                dve.reciprocal(r_den[:, g, :, :], o[:, :, :, HD]).then_inc(den_ready, 1)
                wait(dve, x1_ready, G * n + g)
                dve.wait_ge(den_ready, G * n + g + 1)
                dve.tensor_tensor(pv_scaled[:], o[:, :, :, 0:HD],
                                  r_den[:, g, :, :].unsqueeze(3).to_broadcast([P, TT, R, HD]), ALU.mult)\
                    .then_inc(drained[BANK[f"pv{g}"]], 1)

            def add_values(n, g):
                wait_drained(dve, f"pv{g}", n)
                if g == 0:
                    dve.wait_ge(x1_loaded, 16 * (n + 1))
                part = x1[:, :, g * P:(g + 1) * P].rearrange("p t (r d) -> p t r d", r=R)
                dve.tensor_tensor(part, part, pv_scaled[:], ALU.add).then_inc(x1_ready, 1)

            def attend(n, g):
                scale_values(n, g)
                add_values(n, g)

            def step(i, on):
                p, n, m, l = i + 1, i, i - 1, i - 2

                def gate(t):
                    wait_filled(dve, f"v{t}", i)
                    wait_drained(dve, f"r{t}", i)
                    dve.scalar_tensor_tensor(y[:, t, :], y[:, t, :], 1.0, ps[BANK[f"v{t}"]][:], ALU.add, ALU.mult)\
                        .then_inc(drained[BANK[f"v{t}"]], 1)

                def merge(at):
                    c = MERGE_ORDER[at]
                    dve.scalar_tensor_tensor(tmp[at % 2][:], wqv4[:, c, :], hc[:, c:c + 1], wqv1[:, c, :],
                                             ALU.mult, ALU.add).then_inc(f_ready["weff"], 1)

                def merged_lo(at):
                    dst = weff[MERGE_ORDER[at]]
                    dve.wait_ge(hi_ready["weff"], C * m + at + 1)
                    dve.tensor_tensor(dst[1][:, 0, :], tmp[at % 2][:], dst[0][:, 0, :].bitcast(F32),
                                      ALU.subtract).then_inc(split["weff"], 1)

                if "ffn" in on:
                    wait(dve, out_ready, TT * l)
                    normalise("y", lambda t: y[:, t, :], lambda t: x2[:, t, :], l)
                if "xa" in on:
                    psum_lo("cT", cT, cT_hi, 2, m, i)
                if "ffn" in on:
                    wait_drained(dve, "yT0", i)
                    wait_drained(dve, "yT1", i)
                    token_steps(l)
                if "xa" in on:
                    split_lo("ew", ewT, m)
                if "ffn" in on:
                    wait_tmp(dve, "xk", i)
                    mix("xk", l)
                    split_lo("xk", xkT, l)
                if "att" in on:
                    scale_values(n, 0)
                if "xa" in on:
                    wait_filled(dve, "sim", i)
                    dve.tensor_reduce(neg_max[:], half(ps["T0"][:]), AX.X, ALU.max, negate=True)\
                        .then_inc(neg_max_ready, 1)
                if "att" in on:
                    add_values(n, 0)
                if "ffn" in on:
                    wait_tmp(dve, "xr", i)
                    mix("xr", l)
                if "xa" in on:
                    wait_drained(dve, "sim", i)
                    dve.reciprocal(a_rsum[:], a_sum[:]).then_inc(a_rsum_ready, 1)
                    dve.wait_ge(e_w1_ready, TT * (m + 1))
                    dve.scalar_tensor_tensor(u[:], neg_max[:], -1.0, e_w1[:], ALU.mult, ALU.add).then_inc(u_ready, 1)
                    dve.wait_ge(a_rsum_ready, m + 1)
                    for t in range(TT):
                        dve.tensor_scalar(a[:, t, :], a[:, t, :], a_rsum[:, t:t + 1], None, ALU.mult)\
                            .then_inc(a_normed, 1)
                if "ffn" in on:
                    split_lo("xr", xrT, l)
                    wait_tmp(dve, "ka", i)
                    for h in range(2):
                        wait_drained(dve, f"k{h}", i)
                        dve.tensor_tensor(tmp[h][:], y[:, h, :], y[:, h, :], ALU.mult).then_inc(f_ready["ka"], 1)
                    split_lo("ka", kaT, l)
                if "att" in on:
                    attend(n, 1)
                if "pre" in on:
                    dve.wait_ge(x_loaded, 16 * (p + 1))
                    layernorm_stats("x", x_in, p)
                if "xa" in on:
                    dve.wait_ge(aT_hi, m + 1)
                    dve.tensor_tensor(aT[1], half(ps[BANK["aT"]][:]), aT[0].bitcast(F32), ALU.subtract)\
                        .then_inc(drained[BANK["aT"]], 1)
                if "ffn" in on:
                    gate(0)
                if "xa" in on:
                    wait_filled(dve, "ub", i)
                    dve.tensor_reduce(ub_neg_max[:], ps[BANK["ub"]][:, 0:S], AX.X, ALU.max, negate=True)\
                        .then_inc(ub_max_ready, 1)
                if "att" in on:
                    attend(n, 2)
                if "xa" in on:
                    wait_drained(dve, "ub", i)
                    dve.reciprocal(ub_rsum[:], ub_sum[:]).then_inc(ub_rsum_ready, 1)
                    wait_tmp(dve, "hc", i)
                    dve.wait_ge(ub_rsum_ready, m + 1)
                    for c in range(C):
                        dve.tensor_tensor_reduce(tmp[c // 2][:, (c % 2) * S:(c % 2 + 1) * S], eTf[:, c, :], batt,
                                                 ub_rsum[:], 0.0, ALU.mult, ALU.add, hc[:, c:c + 1])\
                            .then_inc(hc_ready, 1)
                if "ffn" in on:
                    gate(1)
                if "xa" in on:
                    wait_tmp(dve, "eh", i)
                    for h in range(2):
                        bank = BANK[f"hq{h}"]
                        dve.wait_ge(hqT_hi, 2 * m + h + 1)
                        dve.tensor_tensor(hqT[1][:, 2 * h:2 * h + 2, :], half(ps[bank][:]),
                                          hqT[0][:, 2 * h:2 * h + 2, :].bitcast(F32), ALU.subtract)
                        dve.tensor_tensor(tmp[h][:], ps[bank][:], eTf[:, 2 * h:2 * h + 2, :].rearrange(
                            "p c s -> p (c s)"), ALU.mult).then_inc(drained[bank], 1)
                    split_lo("eh", ehT, m)
                if "att" in on:
                    attend(n, 3)
                if "xa" in on:
                    wait_tmp(dve, "weff", i)
                    merge(0)
                    merge(1)
                    for at in range(C):
                        merged_lo(at)
                        if at + 2 < C:
                            dve.wait_ge(split["weff"], C * m + at + 1)
                            merge(at + 2)
                if "pre" in on:
                    if "att" in on:
                        wait_filled(dve, "pv3", i)
                    normalise("x", lambda t: xn[:, t, 0:D], lambda t: x_in[:, t, :], p)
                    psum_lo("xT", xT, xT_hi, 2, p, i)
                if "att" in on:
                    dve.wait_ge(x1_ready, G * (n + 1))
                    layernorm_stats("e", x1, n)
                    if "pre" in on:
                        dve.wait_ge(normed["x"], TT * (p + 1))
                    normalise("e", lambda t: e[:, t, :], lambda t: x1[:, t, :], n)
                    dve.wait_ge(normed["e"], TT * (n + 1))
                    wait_tmp(dve, "e_w1", i)
                    for t in range(TT):
                        dve.tensor_tensor_reduce(tmp[t][:], e[:, t, :], w1_row[:], 1.0, b_sim_col[:], ALU.mult,
                                                 ALU.add, e_w1[:, t:t + 1]).then_inc(e_w1_ready, 1)
                if "xa" in on:
                    wait(dve, out_stored, 16 * TT * m)
                    for t in range(TT):
                        wait_filled(dve, f"h{t}", i)
                        if t == 0:
                            dve.wait_ge(x1b_ready, m + 1)
                        dve.tensor_tensor(x2[:, t, :], ps[BANK[f"h{t}"]][:], x1b[:, t, :], ALU.add)\
                            .then_inc(drained[BANK[f"h{t}"]], 1)
                        wait_drained(dve, f"h{t}", i)
                        dve.bn_stats(stats["y"][:, t, :], x2[:, t, :]).then_inc(stats_done["y"], 1)
                    layernorm_moments("y", m)

            steps(dve, step)

        @block.tensor
        def _(pe):
            def transpose(dst, src, n=P):
                return pe.transpose(dst, src, ident[:])

            def product(dst, lhs, rhs, start, stop):
                return list(passes(dst, lhs, rhs, start, stop))[-1]

            def passes(dst, lhs, rhs, start, stop):
                for n, (x, w) in enumerate(((0, 0), (0, 1), (1, 0))):
                    yield pe.matmul(dst, lhs[x], rhs[w], start=start and n == 0, stop=stop and n == 2)

            def claim(name, i):
                pe.wait_ge(drained[BANK[name]], fill_number(name, i) - 1)
                return ps[BANK[name]]

            def parts(pair, *index):
                return [t[index] for t in pair]

            ALL = slice(None)

            pe.wait_ge(consts_ready, 5)
            for n, name in enumerate(("wkT", "wrT", "wvT")):
                wait_staged(pe, 2 * n)
                wait_staged(pe, 2 * n + 1)
                for kc in range(C):
                    bank = BANKS[kc]
                    wait(pe, drained[bank], n)
                    for dc in range(C):
                        src = stage[(2 * n + dc // 2) % len(stage)][:, dc % 2, kc * P:(kc + 1) * P]
                        last = transpose(ps[bank][:, dc * P:(dc + 1) * P], src)
                    last.then_inc(filled[bank], 1)
                pe.wait_ge(drained[BANKS[-1]], n + 1)
                pe.sem_inc(w_turned, 1)

            def turn(name, src, i):
                for h in range(2):
                    dst = claim(f"{name}{h}", i)
                    for c in range(2 * h, 2 * h + 2):
                        for t in range(TT):
                            at = (c % 2) * S + t * P
                            last = transpose(dst[:, at:at + P], src(t, c))
                    last.then_inc(filled[BANK[f"{name}{h}"]], 1)

            def score_passes(n, g):
                if g:
                    pe.wait_ge(probs_ready, G * n + g)
                else:
                    wait(pe, probs_ready, G * n)
                for k in range(TT):
                    at = slice(k * S, k * S + S - k * P)
                    for nth, (lhs, rhs) in enumerate(((0, 0), (0, 1), (1, 0))):
                        for r in range(R):
                            rows = slice(r * HD, (r + 1) * HD)
                            last = pe.matmul(ps_scores[:, r, at], xT[lhs][rows, g, k * P:(k + 1) * P],
                                             xT[rhs][rows, g, k * P:S], start=nth == 0, stop=nth == 2)
                            if (k, nth, r) == (TT - 1, 2, R - 1):
                                last.then_inc(scores_ready, 1)
                            yield

            def head(k, h):
                v = xn[:, k, h * HD:(h + 1) * HD]
                return bass.AP(tensor=v.tensor, offset=v.offset, ap=[list(v.ap[0]), [D - h * HD, 2], [1, HD]])

            def value_blocks(n, g):
                name = f"pv{g}"
                dst = claim(name, n)
                pe.wait_ge(probs_masked, G * n + g + 1)
                for t in range(TT):
                    for r in range(R):
                        at = (t * R + r) * 2 * HD
                        for k in range(t + 1):
                            cols = slice((k + t) * P, (k + t + 1) * P)
                            last = pe.matmul(dst[:, at:at + 2 * HD], probs[:, r, cols], head(k, g * R + r),
                                             start=k == 0, stop=k == t)
                            if (t, r, k) == (TT - 1, R - 1, t):
                                last.then_inc(filled[BANK[name]], 1)
                            yield

            def go_on(work, count):
                for _ in range(count):
                    next(work, None)

            def finish(work):
                for _ in work:
                    pass

            NOTHING = iter(())

            def tokens_by(name, dst, x, w, t, start=True, stop=True, beside=NOTHING, count=0):
                for c in range(C):
                    for nth, last in enumerate(passes(dst[:], parts(x, ALL, c, slice(t * P, (t + 1) * P)), w(c),
                                                      start and c == 0, stop and c == C - 1)):
                        if stop and (c, nth) == (C - 1, 2):
                            last.then_inc(filled[BANK[name]], 1)
                        go_on(beside, count)

            def step(i, on):
                p, n, m, l = i + 1, i, i - 1, i - 2

                def weighted(name, source, weights, t, beside=NOTHING, count=0):
                    name = f"{name}{t}"
                    tokens_by(name, claim(name, i), source, lambda c: parts(wT[weights], ALL, c, ALL), t,
                              beside=beside, count=count)

                def features(t, lhs, rhs, start, stop, beside=NOTHING, count=0):
                    name = f"h{t}"
                    tokens_by(name, ps[BANK[name]], lhs, rhs, t, start, stop, beside, count)

                if "xa" in on:
                    pe.wait_ge(normed["e"], TT * (m + 1))
                    turn("eT", lambda t, c: e[:, t, c * P:(c + 1) * P], i)
                    pe.wait_ge(ctx_loaded, 16 * (m + 1))
                    turn("cT", lambda t, c: ctx_sb[:, t, c * P:(c + 1) * P], i)
                if "att" in on:
                    finish(score_passes(n, 1))
                if "ffn" in on:
                    pe.wait_ge(normed["y"], TT * (l + 1))
                    turn("yT", lambda t, c: y[:, t, c * P:(c + 1) * P], i)
                if "att" in on:
                    finish(value_blocks(n, 0))
                if "xa" in on:
                    pe.wait_ge(split["ew"], 2 * (m + 1))
                    wait_drained(pe, "cT1", i)
                    dst = claim("sim", i)
                    for t in range(TT):
                        for c in range(C):
                            last = product(dst[:, t * S:(t + 1) * S], parts(ewT, ALL, c, slice(t * P, (t + 1) * P)),
                                           parts(cT, ALL, c, ALL), c == 0, c == C - 1)
                    last.then_inc(filled[BANK["sim"]], 1)
                values1 = value_blocks(n, 1) if "att" in on else NOTHING
                if "ffn" in on:
                    pe.wait_ge(split["xk"], 2 * (l + 1))
                    for h in range(2):
                        dst = claim(f"k{h}", i)
                        for d in range(2 * h, 2 * h + 2):
                            for c in range(C):
                                for nth, last in enumerate(passes(dst[:, (d % 2) * S:(d % 2 + 1) * S],
                                                                  parts(wT["wkT"], ALL, c, slice(d * P, (d + 1) * P)),
                                                                  parts(xkT, ALL, c, ALL), c == 0, c == C - 1)):
                                    if (d, c, nth) == (2 * h + 1, C - 1, 2):
                                        last.then_inc(filled[BANK[f"k{h}"]], 1)
                                    if h and nth % 2 == 0:
                                        go_on(values1, 1)
                finish(values1)
                scores2 = score_passes(n, 2) if "att" in on else NOTHING
                if "ffn" in on:
                    pe.wait_ge(split["xr"], 2 * (l + 1))
                    weighted("r", xrT, "wrT", 0, scores2, 2)
                finish(scores2)
                if "xa" in on:
                    pe.wait_ge(a_normed, TT * (m + 1))
                    dst = claim("aT", i)
                    for j in range(TT):
                        for t in range(TT):
                            last = transpose(dst[:, j * S + t * P:j * S + (t + 1) * P], a[:, t, j * P:(j + 1) * P])
                    last.then_inc(filled[BANK["aT"]], 1)
                if "ffn" in on:
                    pe.wait_ge(split["ka"], 2 * (l + 1))
                    weighted("v", kaT, "wvT", 0)
                if "xa" in on:
                    pe.wait_ge(u_ready, m + 1)
                    dst = claim("ub", i)
                    for t in range(TT):
                        last = pe.matmul(dst[:, t * P:(t + 1) * P], u[:, t:t + 1].to_broadcast([P, P]), ident[:],
                                         start=True, stop=True)
                    last.then_inc(filled[BANK["ub"]], 1)
                values2 = value_blocks(n, 2) if "att" in on else NOTHING
                if "ffn" in on:
                    weighted("r", xrT, "wrT", 1, values2, 1)
                finish(values2)
                scores3 = score_passes(n, 3) if "att" in on else NOTHING
                if "ffn" in on:
                    weighted("v", kaT, "wvT", 1, scores3, 3)
                finish(scores3)
                if "xa" in on:
                    pe.wait_ge(ctx_split, m + 1)
                    wait_drained(pe, "aT", i)
                    for h in range(2):
                        dst = claim(f"hq{h}", i)
                        for c in range(2 * h, 2 * h + 2):
                            for j in range(TT):
                                last = product(dst[:, (c % 2) * S:(c % 2 + 1) * S],
                                               parts(c_rows, ALL, j, slice(c * P, (c + 1) * P)),
                                               parts(aT, ALL, j, ALL), j == 0, j == TT - 1)
                        last.then_inc(filled[BANK[f"hq{h}"]], 1)
                if "att" in on:
                    finish(value_blocks(n, 3))
                if "xa" in on:
                    wait_drained(pe, "hq0", i)
                    wait_drained(pe, "hq1", i)
                    for t in range(TT):
                        features(t, hqT, lambda c: parts(wqv2, ALL, c, ALL), True, False)
                    pe.wait_ge(split["eh"], 2 * (m + 1))
                    for t in range(TT):
                        features(t, ehT, lambda c: parts(wqv3, ALL, c, ALL), False, False)
                if "pre" in on:
                    pe.wait_ge(normed["x"], TT * (p + 1))
                    turn("xT", lambda t, c: xn[:, t, c * P:(c + 1) * P], i)
                if "xa" in on:
                    pe.wait_ge(eT_split, 2 * (m + 1))
                    pe.wait_ge(split["weff"], C * (m + 1))
                    features(0, eT, lambda c: parts(weff[c], ALL, 0, ALL), False, True)
                scores0 = NOTHING
                if "pre" in on:
                    wait_drained(pe, "xT0", i)
                    wait_drained(pe, "xT1", i)
                    scores0 = score_passes(p, 0)
                if "xa" in on:
                    features(1, eT, lambda c: parts(weff[c], ALL, 0, ALL), False, True, scores0, 3)
                finish(scores0)

            steps(pe, step)


_INS = ["x", "ctx_1024", "L0_xattn_w_sim", "L0_xattn_b_sim", "L0_xattn_W_qv", "L0_xattn_b_qv", "L0_ffn_W_r",
        "L0_ffn_W_k", "L0_ffn_W_v", "L0_ffn_mu_r", "L0_ffn_mu_k"]


def kernel(**inputs):
    import numpy as np
    import concourse.bacc as bacc
    from concourse.bass_utils import run_bass_kernel_spmd as run

    nc = bacc.Bacc("TRN2", target_bir_lowering=False, num_devices=1)
    arrays, args = {}, []
    for name in _INS:
        arrays[f"in_{name}"] = np.ascontiguousarray(inputs[name])
        args.append(nc.dram_tensor(f"in_{name}", arrays[f"in_{name}"].shape, F32, kind="ExternalInput").ap())
    args.append(nc.dram_tensor("out", (B, S, D), F32, kind="ExternalOutput").ap())
    build(nc, *args)
    return run(nc, [arrays], core_ids=[0]).results[0]["out"]
```

```python
from contextlib import ExitStack

import concourse.bass as bass
from concourse import mybir

ACT = mybir.ActivationFunctionType
ALU = mybir.AluOpType
AX = mybir.AxisListType
F32 = mybir.dt.float32
F32R = mybir.dt.float32r

P = 128
B, S, D = 32, 256, 512
H = 16
HD = D // H
TT = S // P
C = D // P
G = C
R = H // G
EPS = 1e-5
SCALE = HD ** -0.5
SHIFT = D * SCALE / 2

MERGE_ORDER = [2, 3, 0, 1]
LATE = {"pre": -1, "att": 0, "xa": 1, "ffn": 2}
FILLS = {
    "T0": [("eT0", "xa"), ("yT0", "ffn"), ("sim", "xa"), ("aT", "xa"), ("ub", "xa"),
           ("xT0", "pre")],
    "T1": [("eT1", "xa"), ("yT1", "ffn"), ("pv1", "att"),
           ("pv2", "att"), ("pv3", "att"), ("xT1", "pre")],
    "D0": [("cT0", "xa"), ("k0", "ffn"), ("r0", "ffn"), ("r1", "ffn"), ("hq0", "xa"), ("h0", "xa")],
    "D1": [("cT1", "xa"), ("pv0", "att"), ("k1", "ffn"), ("v0", "ffn"), ("v1", "ffn"), ("hq1", "xa"), ("h1", "xa")],
}
BANK = {name: bank for bank, fills in FILLS.items() for name, _ in fills}
BANKS = list(FILLS)
TMP_USES = [("ew", "xa", "ew", 2, 2), ("xk", "ffn", "xk", 2, 2), ("e_w1", "xa", "e_w1", TT, TT),
            ("xr", "ffn", "xr", 2, 2), ("ka", "ffn", "ka", 2, 2), ("hc", "xa", "hc", C, C), ("eh", "xa", "eh", 2, 2),
            ("weff", "xa", "weff", C, C)]
SETUP_FILLS = {"D0": 6, "D1": 6}


def fill_number(name, i):
    fills = FILLS[BANK[name]]
    at = [f for f, _ in fills].index(name)
    through = [LATE[stage] - (n <= at) for n, (_, stage) in enumerate(fills)]
    if isinstance(i, int):
        return SETUP_FILLS.get(BANK[name], 0) + sum(min(max(i - late, 0), B) for late in through)
    return i * len(fills) + (SETUP_FILLS.get(BANK[name], 0) - sum(through))


def build(nc, x, ctx_in, w_sim, b_sim, w_qv, b_qv, w_r, w_k, w_v, mu_r, mu_k, out):
    with ExitStack() as stack:
        def sb(name, shape, dt=F32):
            return stack.enter_context(nc.sbuf_tensor(name, shape, dt))

        def sem(name):
            return stack.enter_context(nc.semaphore(name))

        ident = sb("ident", [P, P])
        neg_half = sb("neg_half", [P, TT])
        neg_shift = sb("neg_shift", [P, 1])
        w1_row = sb("w1_row", [P, D])
        b_sim_col = sb("b_sim_col", [P, 1])
        b_row = sb("b_row", [P, D])
        w2_col = sb("w2_col", [P, C])
        w3_col = sb("w3_col", [P, C])
        mu = {"xk": sb("mu_k_col", [P, C]), "xr": sb("mu_r_col", [P, C])}
        wqv1 = sb("wqv1", [P, C, D])
        wqv4 = sb("wqv4", [P, C, D])
        wqv2 = [sb(f"wqv2_{h}", [P, C, D], F32R) for h in ("hi", "lo")]
        wqv3 = [sb(f"wqv3_{h}", [P, C, D], F32R) for h in ("hi", "lo")]
        wT = {n: [sb(f"{n}_{h}", [P, C, D], F32R) for h in ("hi", "lo")] for n in ("wrT", "wkT", "wvT")}

        ctx_sb = sb("ctx_sb", [P, TT, D])
        xn = sb("xn", [P, TT, D + HD])
        x1 = sb("x1", [P, TT, D])
        x1b = sb("x1b", [P, TT, D])
        e = sb("e", [P, TT, D])
        x2 = sb("x2", [P, TT, D])
        y = sb("y", [P, TT, D])
        x_in = e
        probs = sb("probs", [P, R, 3 * P])
        pv_scaled = sb("pv_scaled", [P, TT, R, HD])
        tmp = [sb(f"tmp{n}", [P, D]) for n in range(2)]
        eTf = sb("eTf", [P, C, S])
        eT = [sb(f"eT_{h}", [P, C, S], F32R) for h in ("hi", "lo")]
        xT = [sb(f"xT_{h}", [P, C, S], F32R) for h in ("hi", "lo")]
        xT_late = sb("xT_late", [P, C, P])
        yT = sb("yT", [P, C, S + 1])
        a = yT[:, 0:TT, 1:]
        area_c = sb("area_c", [P, 2 * C * S], F32R)
        area_k = sb("area_k", [P, 2 * C * S], F32R)
        area_e = sb("area_e", [P, 2 * C * S], F32R)
        area_x = sb("area_x", [P, 2 * C * S], F32R)
        area_m = sb("area_m", [P, 2 * C * S], F32R)

        def pair(area, n, width, base=0, step=C * S):
            return [area[:, base + h * step:base + h * step + n * width].rearrange("p (c s) -> p c s", c=n)
                    for h in range(2)]

        cT, kaT, ewT, ehT = (pair(t, C, S) for t in (area_c, area_k, area_e, area_e))
        xrT, hqT, xkT = (pair(t, C, S) for t in (area_x, area_x, area_m))
        c_rows = pair(area_m, TT, D)
        aT = pair(area_c, TT, S, step=TT * S)
        weff = [pair((area_c, area_k)[c // 2], 1, D, base=(c % 2) * D) for c in range(C)]

        stats = {n: sb(f"stats_{n}", [P, TT, 6]) for n in "xey"}
        moments = {n: sb(f"moments_{n}", [P, TT, 2]) for n in "xey"}
        var = {n: sb(f"var_{n}", [P, TT]) for n in "xey"}
        rstd = {n: sb(f"rstd_{n}", [P, TT]) for n in "xey"}
        r_den = sb("r_den", [P, G, TT, R])
        e_w1 = sb("e_w1", [P, TT])
        neg_max = sb("neg_max", [P, TT])
        a_sum = sb("a_sum", [P, TT])
        a_rsum = sb("a_rsum", [P, TT])
        u = sb("u", [P, TT])
        ub_neg_max = sb("ub_neg_max", [P, 1])
        ub_sum = sb("ub_sum", [P, 1])
        ub_rsum = sb("ub_rsum", [P, 1])
        batt = a[:, 0, :]
        hc = sb("hc", [P, C])

        ps = {n: stack.enter_context(nc.psum_tensor(n, [P, D], F32)) for n in BANKS}
        ps_scores = stack.enter_context(nc.psum_tensor("ps_scores", [P, R, D], F32))

        filled = {n: sem(f"filled_{n}") for n in BANKS}
        drained = {n: sem(f"drained_{n}") for n in BANKS}

        x_loaded, ctx_loaded, x1_loaded, out_stored = map(sem, ("x_loaded", "ctx_loaded", "x1_loaded", "out_stored"))
        small_loaded, w_turned, w_split, wqv_loaded = map(sem, ("small_loaded", "w_turned", "w_split", "wqv_loaded"))
        stage_loaded = [sem(f"stage_loaded_{n}") for n in range(4)]
        w_hi, consts_ready, ident_zero = map(sem, ("w_hi", "consts_ready", "ident_zero"))
        stats_done = {n: sem(f"stats_done_{n}") for n in "xey"}
        moments_done = {n: sem(f"moments_done_{n}") for n in "xey"}
        var_done = {n: sem(f"var_done_{n}") for n in "xey"}
        rstd_done = {n: sem(f"rstd_done_{n}") for n in "xey"}
        normed = {n: sem(f"normed_{n}") for n in "xey"}
        scores_ready, probs_ready, probs_masked = map(sem, ("scores_ready", "probs_ready", "probs_masked"))
        den_ready, x1_ready, x1b_ready = map(sem, ("den_ready", "x1_ready", "x1b_ready"))
        eT_hi, eT_split, cT_hi, xT_hi, aT_hi, hqT_hi = map(
            sem, ("eT_hi", "eT_split", "cT_hi", "xT_hi", "aT_hi", "hqT_hi"))
        KINDS = ("ew", "xk", "xr", "ka", "eh", "weff")
        f_ready = {n: sem(f"{n}_f") for n in KINDS}
        hi_ready = {n: sem(f"{n}_hi") for n in KINDS}
        split = {n: sem(f"{n}_split") for n in KINDS}
        steps_ready = sem("steps_ready")
        ew_rest_f = sem("ew_rest_f")
        ctx_hi, ctx_split = sem("ctx_hi"), sem("ctx_split")
        pool_passed, dve_passed, sp_passed = map(sem, ("pool_passed", "dve_passed", "sp_passed"))
        out_ready = sem("out_ready")
        neg_max_ready, a_exp, a_rsum_ready, a_normed, e_w1_ready, u_ready = map(
            sem, ("neg_max_ready", "a_exp", "a_rsum_ready", "a_normed", "e_w1_ready", "u_ready"))
        ub_max_ready, ub_rsum_ready, hc_ready = map(sem, ("ub_max_ready", "ub_rsum_ready", "hc_ready"))

        def wait(eng, semaphore, value):
            if not isinstance(value, int) or value > 0:
                eng.wait_ge(semaphore, value)

        def wait_filled(eng, name, i):
            eng.wait_ge(filled[BANK[name]], fill_number(name, i))

        def wait_drained(eng, name, i):
            eng.wait_ge(drained[BANK[name]], fill_number(name, i))

        def stages(i):
            return {n for n, late in LATE.items() if 0 <= i - late < B}

        def wait_tmp(eng, kind, i, part=None):
            tmp_used = {**split, "hc": hc_ready, "e_w1": e_w1_ready}
            at = [use[0] for use in TMP_USES].index(kind)
            for n in range(at - 1, at - 1 - len(TMP_USES), -1):
                _, stage_name, count, upto, per = TMP_USES[n]
                j = i - (n < 0)
                if part is not None and upto == 2:
                    upto = part + 1
                if not isinstance(i, int) or stage_name in stages(j):
                    eng.wait_ge(tmp_used[count], per * (j - LATE[stage_name]) + upto)
                    return

        def half(bank_ap):
            return bank_ap.rearrange("p (c s) -> p c s", c=2)

        def steps(eng, step):
            first = max(LATE.values())
            last = B - 1 + min(LATE.values())
            for i in range(min(LATE.values()), first):
                step(i, stages(i))
            with eng.Fori(first, last + 1) as i:
                step(i, set(LATE))
            for i in range(last + 1, B + max(LATE.values())):
                step(i, stages(i))

        stage = [x1b[:], y[:], x2[:], eTf[:].rearrange("p (h c) s -> p h (c s)", h=2)]
        staged = [(n, h) for n in ("wkT", "wrT", "wvT", "wqv2", "wqv3") for h in range(2)]

        turned = ("wkT", "wrT", "wvT")

        def wait_staged(eng, n):
            eng.wait_ge(stage_loaded[n % len(stage)], 16 * (n // len(stage) + 1))

        def wait_stage_free(eng):
            eng.wait_ge(w_turned, len(turned))
            eng.wait_ge(w_split, len(staged) - 2 * len(turned))

        block = stack.enter_context(nc.Block())

        @block.sync
        def _(sp):
            xv = x.rearrange("b (t p) d -> b p t d", p=P)
            cv = ctx_in.rearrange("b (t p) d -> b p t d", p=P)
            ov = out.rearrange("b (t p) d -> b p t d", p=P)
            wqv = w_qv.rearrange("(q h c p) d -> q h p c d", q=4, h=2, p=P)
            dram = {"wkT": w_k, "wrT": w_r, "wvT": w_v}

            def load_staged(n):
                name, h = staged[n]
                if n >= len(stage):
                    sp.wait_ge(w_turned, (n - len(stage)) // 2 + 1)
                src = dram[name].rearrange("(h c p) d -> h p c d", h=2, p=P)[h] if name in turned else \
                    wqv[int(name[-1]) - 1, h]
                sp.dma_start(stage[n % len(stage)], src).then_inc(stage_loaded[n % len(stage)], 16)

            def step(i, on):
                p, n, m, l = i + 1, i, i - 1, i - 2
                if "pre" in on and "xa" not in on:
                    if p:
                        sp.wait_ge(normed["x"], TT * p)
                    sp.dma_start(x_in[:], xv[p]).then_inc(x_loaded, 16)
                if "att" in on:
                    wait(sp, normed["e"], TT * n)
                    wait(sp, x1b_ready, n)
                    sp.dma_start(x1[:], xv[n]).then_inc(x1_loaded, 16)
                if "pre" in on and "xa" in on:
                    wait_filled(sp, "eT1", i)
                    sp.sem_inc(sp_passed, 1)
                    sp.wait_ge(e_w1_ready, TT * (m + 1))
                    sp.dma_start(x_in[:], xv[p]).then_inc(x_loaded, 16)
                if "xa" in on and not (isinstance(m, int) and m == B - 1):
                    sp.wait_ge(ctx_split, m + 1)
                    sp.dma_start(ctx_sb[:], cv[m + 1]).then_inc(ctx_loaded, 16)
                if "ffn" in on:
                    for t in range(TT):
                        sp.wait_ge(out_ready, TT * l + t + 1)
                        sp.dma_start(ov[l][:, t], x2[:, t, :]).then_inc(out_stored, 16)
                if isinstance(i, int) and i == -1:
                    for n in range(len(stage)):
                        load_staged(n)
                    sp.dma_start(ctx_sb[:], cv[0]).then_inc(ctx_loaded, 16)
                if isinstance(i, int) and i == 0:
                    for n in range(len(stage), len(staged)):
                        load_staged(n)
                    for h in range(2):
                        sp.dma_start(wqv1[:, 2 * h:2 * h + 2, :], wqv[0, h]).then_inc(wqv_loaded, 16)
                        sp.dma_start(wqv4[:, 2 * h:2 * h + 2, :], wqv[3, h]).then_inc(wqv_loaded, 16)

            steps(sp, step)
            sp.wait_ge(out_stored, 16 * TT * B)

        @block.gpsimd
        def _(pool):
            pool.memset(ident[:], 0.0).then_inc(ident_zero, 1)
            pool.memset(neg_half[:], -0.5).then_inc(consts_ready, 1)
            pool.memset(neg_shift[:], -SHIFT).then_inc(consts_ready, 1)
            pool.memset(xn[:, :, D:], 1.0).then_inc(consts_ready, 1)
            pool.memset(yT[:, :, 0:1], 0.0).then_inc(consts_ready, 1)
            pool.wait_ge(ident_zero, 1)
            pool.affine_select(out=ident[:], in_=ident[:], compare_op=ALU.not_equal, fill=1.0, base=0,
                               pattern=[[-1, P]], channel_multiplier=1).then_inc(consts_ready, 1)
            pool.dma_start(w2_col[:], w_sim[D:2 * D].rearrange("(c p) -> p c", p=P),
                           allow_slow_non_contiguous=True).then_inc(small_loaded, 16)
            pool.dma_start(w3_col[:], w_sim[2 * D:3 * D].rearrange("(c p) -> p c", p=P),
                           allow_slow_non_contiguous=True).then_inc(small_loaded, 16)
            pool.dma_start(mu["xr"][:], mu_r.rearrange("(c p) -> p c", p=P),
                           allow_slow_non_contiguous=True).then_inc(small_loaded, 16)
            pool.dma_start(mu["xk"][:], mu_k.rearrange("(c p) -> p c", p=P),
                           allow_slow_non_contiguous=True).then_inc(small_loaded, 16)
            pool.dma_start(w1_row[:], w_sim[0:D].partition_broadcast(P)).then_inc(small_loaded, 16)
            pool.dma_start(b_row[:], b_qv.partition_broadcast(P)).then_inc(small_loaded, 16)
            pool.dma_start(b_sim_col[:], b_sim.partition_broadcast(P)).then_inc(small_loaded, 16)
            pool.wait_ge(consts_ready, 5)

            def root(n, b):
                pool.wait_ge(var_done[n], b + 1)
                pool.tensor_tensor(rstd[n][:], var[n][:], neg_half[:], ALU.pow).then_inc(rstd_done[n], 1)

            def mask(n, g):
                pool.wait_ge(probs_ready, G * n + g + 1)
                pool.sem_inc(pool_passed, 1)
                for k in range(TT):
                    diag = probs[:, :, 2 * k * P:(2 * k + 1) * P]
                    last = pool.affine_select(out=diag, in_=diag, compare_op=ALU.is_ge, fill=0.0, base=0,
                                              pattern=[[0, R], [1, P]], channel_multiplier=-1)
                last.then_inc(probs_masked, 1)

            def add_out(i, l, t):
                wait_drained(pool, f"v{t}", i)
                pool.tensor_tensor(x2[:, t, :], x2[:, t, :], y[:, t, :], ALU.add).then_inc(out_ready, 1)

            def step(i, on):
                p, n, m, l = i + 1, i, i - 1, i - 2
                if isinstance(i, int) and i == 1:
                    pool.wait_ge(small_loaded, 7 * 16)
                if "att" in on:
                    mask(n, 0)
                if "ffn" in on:
                    root("y", l)
                if "xa" in on:
                    for h in range(2):
                        pool.wait_ge(hi_ready["ew"], 2 * m + h + 1)
                        pool.tensor_tensor(ewT[1][:, 2 * h:2 * h + 2, :], half(tmp[h][:]),
                                           ewT[0][:, 2 * h:2 * h + 2, :].bitcast(F32), ALU.subtract)\
                            .then_inc(split["ew"], 1)
                    pool.wait_ge(x1_ready, G * (m + 1))
                    if isinstance(m, int) and m == 0:
                        wait_stage_free(pool)
                    else:
                        wait_drained(pool, "h0", i - 1)
                        wait_drained(pool, "h1", i - 1)
                    for t in range(TT):
                        last = pool.tensor_tensor(x1b[:, t, :], x1[:, t, :], b_row[:], ALU.add)
                    last.then_inc(x1b_ready, 1)
                if "att" in on:
                    mask(n, 1)
                if "xa" in on:
                    for h in range(2):
                        pool.wait_ge(eT_hi, 2 * m + h + 1)
                        pool.tensor_tensor(eT[1][:, 2 * h:2 * h + 2, :], eTf[:, 2 * h:2 * h + 2, :],
                                           eT[0][:, 2 * h:2 * h + 2, :].bitcast(F32), ALU.subtract)\
                            .then_inc(eT_split, 1)
                    pool.wait_ge(ctx_loaded, 16 * (m + 1))
                    wait_filled(pool, "k1" if "ffn" in on else "cT1", i)
                    pool.sem_inc(pool_passed, 1)
                    for t in range(TT):
                        last = pool.tensor_scalar(c_rows[0][:, t, :], ctx_sb[:, t, :], 1.0, 0.0, ALU.mult, ALU.add)
                    last.then_inc(ctx_hi, 1)
                    pool.wait_ge(ctx_hi, m + 1)
                    for t in range(TT):
                        last = pool.tensor_tensor(c_rows[1][:, t, :], ctx_sb[:, t, :],
                                                  c_rows[0][:, t, :].bitcast(F32), ALU.subtract)
                    last.then_inc(ctx_split, 1)
                if "att" in on:
                    mask(n, 2)
                if "pre" in on:
                    root("x", p)
                if "ffn" in on:
                    add_out(i, l, 0)
                if "att" in on:
                    mask(n, 3)
                if "ffn" in on:
                    add_out(i, l, 1)
                if "att" in on:
                    root("e", n)

            steps(pool, step)

        @block.scalar
        def _(act):
            def copy(dst, src):
                return act.activation(dst, src, ACT.Copy)

            def turned_hi(matrix):
                for n in range(matrix * C, (matrix + 1) * C):
                    name, kc, bank = turned[n // C], n % C, f"D{n % 2}"
                    act.wait_ge(filled[bank], n // 2 + 1)
                    act.activation(wT[name][0][:, kc, :], ps[bank][:], ACT.Copy,
                                   scale=0.5 if name == "wvT" else 1.0).then_inc(w_hi, 1)

            def staged_hi():
                for n in range(2 * len(turned), len(staged)):
                    name, h = staged[n]
                    dst = (wqv2 if name == "wqv2" else wqv3)[0]
                    wait_staged(act, n)
                    copy(dst[:, 2 * h:2 * h + 2, :], stage[n % len(stage)]).then_inc(w_hi, 1)

            act.wait_ge(consts_ready, 5)

            def exp_scores(n, g):
                act.wait_ge(scores_ready, G * n + g + 1)
                if g:
                    wait_filled(act, f"pv{g - 1}", n)
                elif not isinstance(n, int) or n > 0:
                    wait_filled(act, f"pv{G - 1}", n - 1)
                act.activation(probs[:], ps_scores[:, :, 0:3 * P], ACT.Exp, bias=neg_shift[:], scale=SCALE)\
                    .then_inc(probs_ready, 1)

            def split_hi(kind, dst, b):
                for h in range(2):
                    act.wait_ge(f_ready[kind], 2 * b + h + 1)
                    copy(dst[0][:, 2 * h:2 * h + 2, :], half(tmp[h][:])).then_inc(hi_ready[kind], 1)

            def psum_hi(name, dst, done, i):
                for h in range(2):
                    wait_filled(act, f"{name}{h}", i)
                    copy(dst[0][:, 2 * h:2 * h + 2, :], half(ps[BANK[f"{name}{h}"]][:])).then_inc(done, 1)

            def step(i, on):
                p, n, m, l = i + 1, i, i - 1, i - 2
                def ew_hi(h):
                    copy(ewT[0][:, 2 * h:2 * h + 2, :], half(tmp[h][:])).then_inc(hi_ready["ew"], 1)

                def merged_hi(at):
                    act.wait_ge(f_ready["weff"], C * m + at + 1)
                    copy(weff[MERGE_ORDER[at]][0][:, 0, :], tmp[at % 2][:]).then_inc(hi_ready["weff"], 1)

                def tanh(t):
                    wait_filled(act, f"r{t}", i)
                    act.activation(y[:, t, :], ps[BANK[f"r{t}"]][:], ACT.Tanh, scale=0.5)\
                        .then_inc(drained[BANK[f"r{t}"]], 1)

                if "att" in on:
                    exp_scores(n, 0)
                first_step = isinstance(i, int) and i == 0
                if first_step:
                    turned_hi(1)
                    turned_hi(2)
                if isinstance(i, int) and i == 1:
                    wait_stage_free(act)
                    act.wait_ge(small_loaded, 7 * 16)
                if "xa" in on:
                    for h in range(2):
                        wait_filled(act, f"eT{h}", i)
                        copy(eTf[:, 2 * h:2 * h + 2, :], half(ps[BANK[f"eT{h}"]][:]))\
                            .then_inc(drained[BANK[f"eT{h}"]], 1)
                if "xa" in on:
                    psum_hi("cT", cT, cT_hi, i)
                    wait_tmp(act, "ew", i)
                    wait_drained(act, "eT0", i)
                    for c in range(2):
                        last = act.activation(half(tmp[0][:])[:, c, :], eTf[:, c, :], ACT.Identity,
                                              bias=w2_col[:, c:c + 1], scale=w3_col[:, c:c + 1])
                    last.then_inc(f_ready["ew"], 1)
                    act.wait_ge(f_ready["ew"], m + 1)
                    ew_hi(0)
                def copy_yT(h):
                    wait_filled(act, f"yT{h}", i)
                    copy(yT[:, 2 * h:2 * h + 2, 1:], half(ps[BANK[f"yT{h}"]][:])).then_inc(drained[BANK[f"yT{h}"]], 1)

                if "ffn" in on:
                    copy_yT(0)
                if "xa" in on:
                    act.wait_ge(ew_rest_f, m + 1)
                    ew_hi(1)
                if "ffn" in on:
                    copy_yT(1)
                if "ffn" in on:
                    split_hi("xk", xkT, l)
                if "att" in on:
                    exp_scores(n, 1)
                if "xa" in on:
                    wait_drained(act, "eT1", i)
                    for h in range(2):
                        copy(eT[0][:, 2 * h:2 * h + 2, :], eTf[:, 2 * h:2 * h + 2, :]).then_inc(eT_hi, 1)
                if "ffn" in on:
                    split_hi("xr", xrT, l)
                if "xa" in on:
                    wait_filled(act, "sim", i)
                    act.wait_ge(neg_max_ready, m + 1)
                    for t in range(TT):
                        last = act.activation(a[:, t, :], ps["T0"][:, t * S:(t + 1) * S], ACT.Exp,
                                              bias=neg_max[:, t:t + 1], accum_out=a_sum[:, t:t + 1])
                        last.then_inc(a_exp if t == 0 else drained[BANK["sim"]], 1)
                if "ffn" in on:
                    for h in range(2):
                        wait_filled(act, f"k{h}", i)
                        act.activation(y[:, h, :], ps[BANK[f"k{h}"]][:], ACT.Relu).then_inc(drained[BANK[f"k{h}"]], 1)
                    split_hi("ka", kaT, l)
                if "att" in on:
                    exp_scores(n, 2)
                if "xa" in on:
                    wait_filled(act, "aT", i)
                    copy(aT[0], half(ps[BANK["aT"]][:])).then_inc(aT_hi, 1)
                if "ffn" in on:
                    tanh(0)
                if "xa" in on:
                    act.wait_ge(ub_max_ready, m + 1)
                    act.activation(batt, ps[BANK["ub"]][:, 0:S], ACT.Exp, bias=ub_neg_max[:],
                                   accum_out=ub_sum[:]).then_inc(drained[BANK["ub"]], 1)
                if "ffn" in on:
                    tanh(1)
                if "att" in on:
                    exp_scores(n, 3)
                if first_step:
                    staged_hi()
                if "xa" in on:
                    psum_hi("hq", hqT, hqT_hi, i)
                    for h in range(2):
                        wait_drained(act, f"hq{h}", i)
                        copy(ehT[0][:, 2 * h:2 * h + 2, :], half(tmp[h][:])).then_inc(hi_ready["eh"], 1)
                    for at in range(C):
                        merged_hi(at)
                if "pre" in on:
                    for h in range(2):
                        wait_filled(act, f"xT{h}", i)
                        src = half(ps[BANK[f"xT{h}"]][:])
                        copy(xT_late[:, 2 * h:2 * h + 2, :], src[:, :, P:])
                        copy(xT[0][:, 2 * h:2 * h + 2, :], src).then_inc(xT_hi, 1)
                if isinstance(i, int) and i == -1:
                    turned_hi(0)

            steps(act, step)

        @block.vector
        def _(dve):
            def turned_lo(matrix):
                for n in range(matrix * C, (matrix + 1) * C):
                    name, kc, bank = turned[n // C], n % C, f"D{n % 2}"
                    dve.wait_ge(w_hi, n + 1)
                    dve.scalar_tensor_tensor(wT[name][1][:, kc, :], ps[bank][:], 0.5 if name == "wvT" else 1.0,
                                             wT[name][0][:, kc, :].bitcast(F32), ALU.mult, ALU.subtract)\
                        .then_inc(drained[bank], 1)

            def staged_lo():
                for n in range(2 * len(turned), len(staged)):
                    name, h = staged[n]
                    dst = wqv2 if name == "wqv2" else wqv3
                    dve.wait_ge(w_hi, C * len(turned) + n - 2 * len(turned) + 1)
                    dve.tensor_tensor(dst[1][:, 2 * h:2 * h + 2, :], stage[n % len(stage)],
                                      dst[0][:, 2 * h:2 * h + 2, :].bitcast(F32), ALU.subtract).then_inc(w_split, 1)


            def psum_lo(name, dst, done, per, b, i, halves=range(2)):
                for h in halves:
                    bank = BANK[f"{name}{h}"]
                    dve.wait_ge(done, per * b + h + 1)
                    dve.tensor_tensor(dst[1][:, 2 * h:2 * h + 2, :], half(ps[bank][:]),
                                      dst[0][:, 2 * h:2 * h + 2, :].bitcast(F32), ALU.subtract)\
                        .then_inc(drained[bank], 1)

            def split_lo(kind, dst, b):
                for h in range(2):
                    dve.wait_ge(hi_ready[kind], 2 * b + h + 1)
                    dve.tensor_tensor(dst[1][:, 2 * h:2 * h + 2, :], half(tmp[h][:]),
                                      dst[0][:, 2 * h:2 * h + 2, :].bitcast(F32), ALU.subtract)\
                        .then_inc(split[kind], 1)

            def layernorm_stats(n, src, b):
                for t in range(TT):
                    dve.bn_stats(stats[n][:, t, :], src[:, t, :]).then_inc(stats_done[n], 1)
                layernorm_moments(n, b)

            def layernorm_moments(n, b):
                dve.wait_ge(stats_done[n], TT * (b + 1))
                dve.sem_inc(dve_passed, 1)
                for t in range(TT):
                    dve.bn_aggr(moments[n][:, t, :], stats[n][:, t, :]).then_inc(moments_done[n], 1)
                dve.wait_ge(moments_done[n], TT * (b + 1))
                dve.tensor_scalar(var[n][:], moments[n][:, :, 1], EPS, None, ALU.add).then_inc(var_done[n], 1)

            def normalise(n, dst, src, b):
                dve.wait_ge(rstd_done[n], b + 1)
                for t in range(TT):
                    dve.tensor_scalar(dst(t), src(t), moments[n][:, t, 0:1], rstd[n][:, t:t + 1],
                                      ALU.subtract, ALU.mult).then_inc(normed[n], 1)

            def token_steps(b, i):
                wait_filled(dve, "yT1", i)
                for h in range(2):
                    wait_drained(dve, f"yT{h}", i)
                    dve.tensor_tensor(half(y[:, h, :]), yT[:, 2 * h:2 * h + 2, 1:], yT[:, 2 * h:2 * h + 2, 0:S],
                                      ALU.subtract).then_inc(steps_ready, 1)

            def mix(kind, b, i):
                for h in range(2):
                    dve.wait_ge(steps_ready, 2 * b + h + 1)
                    wait_tmp(dve, kind, i, h)
                    for c in range(2 * h, 2 * h + 2):
                        last = dve.scalar_tensor_tensor(half(tmp[h][:])[:, c % 2, :], half(y[:, h, :])[:, c % 2, :],
                                                        mu[kind][:, c:c + 1], yT[:, c, 0:S], ALU.mult, ALU.add)
                    last.then_inc(f_ready[kind], 1)

            def scale_values(n, g):
                wait_filled(dve, f"pv{g}", n)
                o = ps[BANK[f"pv{g}"]][:].rearrange("p (t r d) -> p t r d", t=TT, r=R)
                dve.reciprocal(r_den[:, g, :, :], o[:, :, :, HD]).then_inc(den_ready, 1)
                wait(dve, x1_ready, G * n + g)
                dve.wait_ge(den_ready, G * n + g + 1)
                dve.tensor_tensor(pv_scaled[:], o[:, :, :, 0:HD],
                                  r_den[:, g, :, :].unsqueeze(3).to_broadcast([P, TT, R, HD]), ALU.mult)\
                    .then_inc(drained[BANK[f"pv{g}"]], 1)

            def add_values(n, g):
                wait_drained(dve, f"pv{g}", n)
                if g == 0:
                    dve.wait_ge(x1_loaded, 16 * (n + 1))
                part = x1[:, :, g * P:(g + 1) * P].rearrange("p t (r d) -> p t r d", r=R)
                dve.tensor_tensor(part, part, pv_scaled[:], ALU.add).then_inc(x1_ready, 1)

            def attend(n, g):
                scale_values(n, g)
                add_values(n, g)

            def step(i, on):
                p, n, m, l = i + 1, i, i - 1, i - 2
                if isinstance(i, int) and i == 1:
                    dve.wait_ge(small_loaded, 7 * 16)

                def gate(t):
                    wait_filled(dve, f"v{t}", i)
                    wait_drained(dve, f"r{t}", i)
                    dve.scalar_tensor_tensor(y[:, t, :], y[:, t, :], 1.0, ps[BANK[f"v{t}"]][:], ALU.add, ALU.mult)\
                        .then_inc(drained[BANK[f"v{t}"]], 1)

                def merge(at):
                    c = MERGE_ORDER[at]
                    dve.scalar_tensor_tensor(tmp[at % 2][:], wqv4[:, c, :], hc[:, c:c + 1], wqv1[:, c, :],
                                             ALU.mult, ALU.add).then_inc(f_ready["weff"], 1)

                def merged_lo(at):
                    dst = weff[MERGE_ORDER[at]]
                    dve.wait_ge(hi_ready["weff"], C * m + at + 1)
                    dve.tensor_tensor(dst[1][:, 0, :], tmp[at % 2][:], dst[0][:, 0, :].bitcast(F32),
                                      ALU.subtract).then_inc(split["weff"], 1)

                if "ffn" in on:
                    wait(dve, out_ready, TT * l)
                    normalise("y", lambda t: y[:, t, :], lambda t: x2[:, t, :], l)
                if "xa" in on:
                    psum_lo("cT", cT, cT_hi, 2, m, i, [1])
                    wait_tmp(dve, "ew", i)
                    wait_drained(dve, "eT1", i)
                    for c in range(2, C):
                        last = dve.tensor_scalar(half(tmp[1][:])[:, c % 2, :], eTf[:, c, :], w3_col[:, c:c + 1],
                                                 w2_col[:, c:c + 1], ALU.mult, ALU.add)
                    last.then_inc(ew_rest_f, 1)
                    psum_lo("cT", cT, cT_hi, 2, m, i, [0])
                if "ffn" in on:
                    token_steps(l, i)
                if "ffn" in on:
                    mix("xk", l, i)
                    split_lo("xk", xkT, l)
                first_step = isinstance(i, int) and i == 0
                if isinstance(i, int) and i == 1:
                    wait_stage_free(dve)
                    dve.wait_ge(wqv_loaded, 4 * 16)
                if first_step:
                    turned_lo(1)
                    turned_lo(2)
                if "att" in on:
                    scale_values(n, 0)
                if "xa" in on:
                    wait_tmp(dve, "e_w1", i)
                    dve.wait_ge(normed["e"], TT * (m + 1))
                    for t in range(TT):
                        dve.tensor_tensor_reduce(tmp[t][:], e[:, t, :], w1_row[:], 1.0, b_sim_col[:], ALU.mult,
                                                 ALU.add, e_w1[:, t:t + 1]).then_inc(e_w1_ready, 1)
                    wait_filled(dve, "sim", i)
                    dve.tensor_reduce(neg_max[:], half(ps["T0"][:]), AX.X, ALU.max, negate=True)\
                        .then_inc(neg_max_ready, 1)
                if "att" in on:
                    add_values(n, 0)
                if "ffn" in on:
                    mix("xr", l, i)
                if "ffn" in on:
                    split_lo("xr", xrT, l)
                if "xa" in on:
                    wait_drained(dve, "sim", i)
                    dve.reciprocal(a_rsum[:], a_sum[:]).then_inc(a_rsum_ready, 1)
                    dve.wait_ge(e_w1_ready, TT * (m + 1))
                    dve.scalar_tensor_tensor(u[:], neg_max[:], -1.0, e_w1[:], ALU.mult, ALU.add).then_inc(u_ready, 1)
                    dve.wait_ge(a_rsum_ready, m + 1)
                    for t in range(TT):
                        dve.tensor_scalar(a[:, t, :], a[:, t, :], a_rsum[:, t:t + 1], None, ALU.mult)\
                            .then_inc(a_normed, 1)
                if "ffn" in on:
                    wait_tmp(dve, "ka", i)
                    for h in range(2):
                        wait_drained(dve, f"k{h}", i)
                        dve.tensor_tensor(tmp[h][:], y[:, h, :], y[:, h, :], ALU.mult).then_inc(f_ready["ka"], 1)
                    split_lo("ka", kaT, l)
                if "att" in on:
                    attend(n, 1)
                if "pre" in on:
                    dve.wait_ge(x_loaded, 16 * (p + 1))
                    layernorm_stats("x", x_in, p)
                if "xa" in on:
                    dve.wait_ge(aT_hi, m + 1)
                    dve.tensor_tensor(aT[1], half(ps[BANK["aT"]][:]), aT[0].bitcast(F32), ALU.subtract)\
                        .then_inc(drained[BANK["aT"]], 1)
                if "ffn" in on:
                    gate(0)
                if "xa" in on:
                    wait_filled(dve, "ub", i)
                    dve.tensor_reduce(ub_neg_max[:], ps[BANK["ub"]][:, 0:S], AX.X, ALU.max, negate=True)\
                        .then_inc(ub_max_ready, 1)
                if "att" in on:
                    attend(n, 2)
                if "xa" in on:
                    wait_drained(dve, "ub", i)
                    dve.reciprocal(ub_rsum[:], ub_sum[:]).then_inc(ub_rsum_ready, 1)
                    wait_tmp(dve, "hc", i)
                    dve.wait_ge(ub_rsum_ready, m + 1)
                    for c in range(C):
                        dve.tensor_tensor_reduce(tmp[c // 2][:, (c % 2) * S:(c % 2 + 1) * S], eTf[:, c, :], batt,
                                                 ub_rsum[:], 0.0, ALU.mult, ALU.add, hc[:, c:c + 1])\
                            .then_inc(hc_ready, 1)
                if "ffn" in on:
                    gate(1)
                if "xa" in on:
                    wait_tmp(dve, "eh", i)
                    for h in range(2):
                        bank = BANK[f"hq{h}"]
                        dve.wait_ge(hqT_hi, 2 * m + h + 1)
                        dve.tensor_tensor(hqT[1][:, 2 * h:2 * h + 2, :], half(ps[bank][:]),
                                          hqT[0][:, 2 * h:2 * h + 2, :].bitcast(F32), ALU.subtract)
                        dve.tensor_tensor(tmp[h][:], ps[bank][:], eTf[:, 2 * h:2 * h + 2, :].rearrange(
                            "p c s -> p (c s)"), ALU.mult).then_inc(drained[bank], 1)
                    split_lo("eh", ehT, m)
                if first_step:
                    staged_lo()
                if "att" in on:
                    attend(n, 3)
                if "xa" in on:
                    wait_tmp(dve, "weff", i)
                    merge(0)
                    merge(1)
                    for at in range(C):
                        merged_lo(at)
                        if at + 2 < C:
                            dve.wait_ge(split["weff"], C * m + at + 1)
                            merge(at + 2)
                if "pre" in on:
                    if "att" in on:
                        wait_filled(dve, "pv3", i)
                    normalise("x", lambda t: xn[:, t, 0:D], lambda t: x_in[:, t, :], p)
                    psum_lo("xT", xT, xT_hi, 2, p, i)
                if isinstance(i, int) and i == -1:
                    turned_lo(0)
                if "att" in on:
                    dve.wait_ge(x1_ready, G * (n + 1))
                    layernorm_stats("e", x1, n)

                def add_features(t):
                    wait_filled(dve, f"h{t}", i)
                    dve.tensor_tensor(x2[:, t, :], ps[BANK[f"h{t}"]][:], x1b[:, t, :], ALU.add)\
                        .then_inc(drained[BANK[f"h{t}"]], 1)

                def stats_y(t):
                    wait_drained(dve, f"h{t}", i)
                    dve.bn_stats(stats["y"][:, t, :], x2[:, t, :]).then_inc(stats_done["y"], 1)

                if "xa" in on:
                    wait(dve, out_stored, 16 * TT * m)
                    dve.wait_ge(x1b_ready, m + 1)
                    add_features(0)
                if "att" in on:
                    if "pre" in on:
                        dve.wait_ge(normed["x"], TT * (p + 1))
                    if "xa" in on:
                        dve.wait_ge(e_w1_ready, TT * (m + 1))
                    normalise("e", lambda t: e[:, t, :], lambda t: x1[:, t, :], n)
                if "xa" in on:
                    stats_y(0)
                    add_features(1)
                    stats_y(1)
                    layernorm_moments("y", m)

            steps(dve, step)

        @block.tensor
        def _(pe):
            def transpose(dst, src):
                return pe.transpose(dst, src, ident[:])

            def product(dst, lhs, rhs, start, stop):
                return list(passes(dst, lhs, rhs, start, stop))[-1]

            def passes(dst, lhs, rhs, start, stop):
                for n, (x, w) in enumerate(((0, 0), (0, 1), (1, 0))):
                    yield pe.matmul(dst, lhs[x], rhs[w], start=start and n == 0, stop=stop and n == 2)

            def claim(name, i):
                pe.wait_ge(drained[BANK[name]], fill_number(name, i) - 1)
                return ps[BANK[name]]

            def parts(pair, *index):
                return [t[index] for t in pair]

            ALL = slice(None)

            pe.wait_ge(consts_ready, 5)

            def turn_weights(matrix):
                wait_staged(pe, 2 * matrix)
                wait_staged(pe, 2 * matrix + 1)
                for n in range(matrix * C, (matrix + 1) * C):
                    kc, bank = n % C, f"D{n % 2}"
                    wait(pe, drained[bank], n // 2)
                    for dc in range(C):
                        src = stage[(2 * matrix + dc // 2) % len(stage)][:, dc % 2, kc * P:(kc + 1) * P]
                        last = transpose(ps[bank][:, dc * P:(dc + 1) * P], src)
                    last.then_inc(filled[bank], 1)
                pe.wait_ge(filled[bank], n // 2 + 1)
                pe.sem_inc(w_turned, 1)

            def turn(name, src, i):
                for h in range(2):
                    dst = claim(f"{name}{h}", i)
                    for c in range(2 * h, 2 * h + 2):
                        for t in range(TT):
                            at = (c % 2) * S + t * P
                            last = transpose(dst[:, at:at + P], src(t, c))
                    last.then_inc(filled[BANK[f"{name}{h}"]], 1)

            def score_passes(n, g):
                if g:
                    pe.wait_ge(probs_ready, G * n + g)
                else:
                    wait(pe, probs_ready, G * n)
                for nth, (lhs, rhs) in enumerate(((0, 0), (0, 1), (1, 0))):
                    for r in range(R):
                        rows = slice(r * HD, (r + 1) * HD)
                        pe.matmul(ps_scores[:, r, 0:S], xT[lhs][rows, g, 0:P], xT[rhs][rows, g, :],
                                  start=nth == 0, stop=nth == 2)
                        yield
                for r in range(R):
                    late = xT_late[r * HD:(r + 1) * HD, g, :]
                    last = pe.matmul(ps_scores[:, r, S:S + P], late, late, start=True, stop=True)
                    if r == R - 1:
                        last.then_inc(scores_ready, 1)
                    yield

            def head(k, h):
                v = xn[:, k, h * HD:(h + 1) * HD]
                return bass.AP(tensor=v.tensor, offset=v.offset, ap=[list(v.ap[0]), [D - h * HD, 2], [1, HD]])

            def value_blocks(n, g):
                name = f"pv{g}"
                dst = claim(name, n)
                pe.wait_ge(probs_masked, G * n + g + 1)
                for t in range(TT):
                    for r in range(R):
                        at = (t * R + r) * 2 * HD
                        for k in range(t + 1):
                            cols = slice((k + t) * P, (k + t + 1) * P)
                            last = pe.matmul(dst[:, at:at + 2 * HD], probs[:, r, cols], head(k, g * R + r),
                                             start=k == 0, stop=k == t)
                            if (t, r, k) == (TT - 1, R - 1, t):
                                last.then_inc(filled[BANK[name]], 1)
                            yield

            def go_on(work, count):
                for _ in range(count):
                    next(work, None)

            def finish(work):
                for _ in work:
                    pass

            NOTHING = iter(())

            def tokens_by(name, dst, x, w, t, start=True, stop=True, beside=NOTHING, count=0):
                for c in range(C):
                    for nth, last in enumerate(passes(dst[:], parts(x, ALL, c, slice(t * P, (t + 1) * P)), w(c),
                                                      start and c == 0, stop and c == C - 1)):
                        if stop and (c, nth) == (C - 1, 2):
                            last.then_inc(filled[BANK[name]], 1)
                        go_on(beside, count)

            def step(i, on):
                p, n, m, l = i + 1, i, i - 1, i - 2

                def broadcast_u():
                    pe.wait_ge(u_ready, m + 1)
                    dst = claim("ub", i)
                    for t in range(TT):
                        last = pe.matmul(dst[:, t * P:(t + 1) * P], u[:, t:t + 1].to_broadcast([P, P]), ident[:],
                                         start=True, stop=True)
                    last.then_inc(filled[BANK["ub"]], 1)

                def weighted(name, source, weights, t, beside=NOTHING, count=0):
                    name = f"{name}{t}"
                    tokens_by(name, claim(name, i), source, lambda c: parts(wT[weights], ALL, c, ALL), t,
                              beside=beside, count=count)

                def features(t, lhs, rhs, start, stop, beside=NOTHING, count=0):
                    name = f"h{t}"
                    tokens_by(name, ps[BANK[name]], lhs, rhs, t, start, stop, beside, count)

                if "xa" in on:
                    pe.wait_ge(normed["e"], TT * (m + 1))
                    turn("eT", lambda t, c: e[:, t, c * P:(c + 1) * P], i)
                    pe.wait_ge(ctx_loaded, 16 * (m + 1))
                    turn("cT", lambda t, c: ctx_sb[:, t, c * P:(c + 1) * P], i)
                if "att" in on:
                    finish(score_passes(n, 1))
                if "ffn" in on:
                    pe.wait_ge(normed["y"], TT * (l + 1))
                    turn("yT", lambda t, c: y[:, t, c * P:(c + 1) * P], i)
                first_step = isinstance(i, int) and i == 0
                if first_step:
                    turn_weights(2)
                if "att" in on:
                    finish(value_blocks(n, 0))
                if "xa" in on:
                    pe.wait_ge(split["ew"], 2 * (m + 1))
                    wait_drained(pe, "cT0", i)
                    wait_drained(pe, "cT1", i)
                    dst = claim("sim", i)
                    for t in range(TT):
                        for c in range(C):
                            last = product(dst[:, t * S:(t + 1) * S], parts(ewT, ALL, c, slice(t * P, (t + 1) * P)),
                                           parts(cT, ALL, c, ALL), c == 0, c == C - 1)
                    last.then_inc(filled[BANK["sim"]], 1)
                values1 = value_blocks(n, 1) if "att" in on else NOTHING
                if "ffn" in on:
                    pe.wait_ge(split["xk"], 2 * (l + 1))
                    for h in range(2):
                        dst = claim(f"k{h}", i)
                        for d in range(2 * h, 2 * h + 2):
                            for c in range(C):
                                for nth, last in enumerate(passes(dst[:, (d % 2) * S:(d % 2 + 1) * S],
                                                                  parts(wT["wkT"], ALL, c, slice(d * P, (d + 1) * P)),
                                                                  parts(xkT, ALL, c, ALL), c == 0, c == C - 1)):
                                    if (d, c, nth) == (2 * h + 1, C - 1, 2):
                                        last.then_inc(filled[BANK[f"k{h}"]], 1)
                                    if h and nth % 2 == 0:
                                        go_on(values1, 1)
                scores2 = score_passes(n, 2) if "att" in on else NOTHING
                if "ffn" not in on:
                    finish(scores2)
                finish(values1)
                if "ffn" in on:
                    pe.wait_ge(split["xr"], 2 * (l + 1))
                    weighted("r", xrT, "wrT", 0, scores2, 2)
                finish(scores2)
                if "xa" in on:
                    pe.wait_ge(a_normed, TT * (m + 1))
                    dst = claim("aT", i)
                    for j in range(TT):
                        for t in range(TT):
                            last = transpose(dst[:, j * S + t * P:j * S + (t + 1) * P], a[:, t, j * P:(j + 1) * P])
                    last.then_inc(filled[BANK["aT"]], 1)
                if "ffn" in on:
                    pe.wait_ge(split["ka"], 2 * (l + 1))
                    weighted("v", kaT, "wvT", 0)
                if "xa" in on and "ffn" in on:
                    broadcast_u()
                values2 = value_blocks(n, 2) if "att" in on else NOTHING
                if "ffn" in on:
                    weighted("r", xrT, "wrT", 1, values2, 1)
                scores3 = score_passes(n, 3) if "att" in on else NOTHING
                if "ffn" not in on:
                    finish(scores3)
                finish(values2)
                if "ffn" in on:
                    weighted("v", kaT, "wvT", 1, scores3, 2)
                finish(scores3)
                if "xa" in on:
                    if "ffn" not in on:
                        broadcast_u()
                    pe.wait_ge(ctx_split, m + 1)
                    wait_drained(pe, "aT", i)
                    for h in range(2):
                        dst = claim(f"hq{h}", i)
                        for c in range(2 * h, 2 * h + 2):
                            for j in range(TT):
                                last = product(dst[:, (c % 2) * S:(c % 2 + 1) * S],
                                               parts(c_rows, ALL, j, slice(c * P, (c + 1) * P)),
                                               parts(aT, ALL, j, ALL), j == 0, j == TT - 1)
                        last.then_inc(filled[BANK[f"hq{h}"]], 1)
                if "att" in on:
                    finish(value_blocks(n, 3))
                if "xa" in on:
                    wait_drained(pe, "hq0", i)
                    wait_drained(pe, "hq1", i)
                    for t in range(TT):
                        features(t, hqT, lambda c: parts(wqv2, ALL, c, ALL), True, False)
                    pe.wait_ge(split["eh"], 2 * (m + 1))
                    for t in range(TT):
                        features(t, ehT, lambda c: parts(wqv3, ALL, c, ALL), False, False)
                if "pre" in on:
                    pe.wait_ge(normed["x"], TT * (p + 1))
                    turn("xT", lambda t, c: xn[:, t, c * P:(c + 1) * P], i)
                if "xa" in on:
                    pe.wait_ge(eT_split, 2 * (m + 1))
                    pe.wait_ge(split["weff"], C * (m + 1))
                    features(0, eT, lambda c: parts(weff[c], ALL, 0, ALL), False, True)
                if isinstance(i, int) and i == -1:
                    turn_weights(0)
                scores0 = NOTHING
                if "pre" in on:
                    wait_drained(pe, "xT0", i)
                    wait_drained(pe, "xT1", i)
                    scores0 = score_passes(p, 0)
                if "xa" in on:
                    features(1, eT, lambda c: parts(weff[c], ALL, 0, ALL), False, True, scores0, 2)
                finish(scores0)
                if isinstance(i, int) and i == -1:
                    turn_weights(1)

            steps(pe, step)


_INS = ["x", "ctx_1024", "L0_xattn_w_sim", "L0_xattn_b_sim", "L0_xattn_W_qv", "L0_xattn_b_qv", "L0_ffn_W_r",
        "L0_ffn_W_k", "L0_ffn_W_v", "L0_ffn_mu_r", "L0_ffn_mu_k"]


def kernel(**inputs):
    import numpy as np
    import concourse.bacc as bacc
    from concourse.bass_utils import run_bass_kernel_spmd as run

    nc = bacc.Bacc("TRN2", target_bir_lowering=False, num_devices=1)
    arrays, args = {}, []
    for name in _INS:
        arrays[f"in_{name}"] = np.ascontiguousarray(inputs[name])
        args.append(nc.dram_tensor(f"in_{name}", arrays[f"in_{name}"].shape, F32, kind="ExternalInput").ap())
    args.append(nc.dram_tensor("out", (B, S, D), F32, kind="ExternalOutput").ap())
    build(nc, *args)
    return run(nc, [arrays], core_ids=[0]).results[0]["out"]
```
